# Optimizing a Trainium2 kernel written in Bass

```python
import numpy as np
import jax
import jax.numpy as jnp

def _softmax(x, axis=-1):
    return jax.nn.softmax(x, axis=axis)

def _gelu(x):
    return jax.nn.gelu(x, approximate=True)

def _silu(x):
    return jax.nn.silu(x)

def _sigmoid(x):
    return jax.nn.sigmoid(x)

def _layernorm(x, axis=-1, eps=1e-05):
    m = jnp.mean(x, axis=axis, keepdims=True)
    v = jnp.var(x, axis=axis, keepdims=True)
    return (x - m) / jnp.sqrt(v + eps)

def _scatter_add(tgt, idx, src, axis=0):
    return tgt.at[idx].add(src)

def _segment_sum(src, seg, n):
    return jax.ops.segment_sum(src, seg, n)
kernel_name = 'mk_macaron_d1_jaxref_r8_34c978'

def setup_inputs(seed: int=0):
    np.random.seed(seed)
    _w = jnp.asarray

    def _L0_attn_setup():
        import jax, jax.numpy as jnp
        import numpy as np
        D_MODEL = 128
        THRESH = 0.01
        key = jax.random.key(seed)
        kx, kw = jax.random.split(key)
        x = jax.random.normal(kx, (4, 256, D_MODEL), dtype=jnp.float32)
        W = jax.random.normal(kw, (D_MODEL, D_MODEL), dtype=jnp.float32) / np.sqrt(D_MODEL)
        return {'x': x, 'W': W}
    _L0_attn_in = _L0_attn_setup()

    def _L0_ffn_setup():
        import jax, jax.numpy as jnp
        import numpy as np
        B, S, D, H, E, K = (4, 256, 128, 512, 4, 2)
        key = jax.random.key(seed)
        ks = jax.random.split(key, 7)
        s1 = 1.0 / np.sqrt(D)
        s2 = 1.0 / np.sqrt(H)
        return {'x': jax.random.normal(ks[0], (B, S, D), jnp.float32), 'w1': jax.random.uniform(ks[1], (E, D, H), jnp.float32, -s1, s1), 'b1': jax.random.uniform(ks[2], (E, H), jnp.float32, -s1, s1), 'w2': jax.random.uniform(ks[3], (E, H, D), jnp.float32, -s2, s2), 'b2': jax.random.uniform(ks[4], (E, D), jnp.float32, -s2, s2), 'wr': jax.random.uniform(ks[5], (D, E), jnp.float32, -s1, s1), 'br': jax.random.uniform(ks[6], (E,), jnp.float32, -s1, s1)}
    _L0_ffn_in = _L0_ffn_setup()
    _d = {'L0_attn_x': _L0_attn_in['x'], 'L0_attn_W': _L0_attn_in['W'], 'L0_ffn_w1': _L0_ffn_in['w1'], 'L0_ffn_b1': _L0_ffn_in['b1'], 'L0_ffn_w2': _L0_ffn_in['w2'], 'L0_ffn_b2': _L0_ffn_in['b2'], 'L0_ffn_wr': _L0_ffn_in['wr'], 'L0_ffn_br': _L0_ffn_in['br']}
    _x0 = _d['L0_attn_x']
    _d['L0_attn_x'] = jax.random.normal(jax.random.fold_in(jax.random.key(seed), 1), (2, 1024, 128), dtype=_x0.dtype)
    del _x0
    return _d

def reference(L0_attn_x, L0_attn_W, L0_ffn_w1, L0_ffn_b1, L0_ffn_w2, L0_ffn_b2, L0_ffn_wr, L0_ffn_br):

    def _L0_attn_ref(x, W):
        import jax, jax.numpy as jnp
        import numpy as np
        D_MODEL = 128
        THRESH = 0.01
        B, T, D = x.shape
        scale = 1.0 / jnp.sqrt(jnp.asarray(D, x.dtype))
        scores = jnp.einsum('btd,bsd->bts', x, x) * scale
        probs = jax.nn.softmax(scores, axis=-1)
        vacuum_mask = probs < THRESH
        vacuum_energy = jnp.where(vacuum_mask, probs, 0.0)
        vac_sum = vacuum_energy.sum(axis=-1, keepdims=True)
        vac_in = jnp.broadcast_to(vac_sum, (B, T, D))
        casimir = jnp.einsum('btd,od->bto', vac_in, W)
        sparse_probs = jnp.where(vacuum_mask, 0.0, probs)
        sparse_probs = sparse_probs / (sparse_probs.sum(axis=-1, keepdims=True) + 1e-09)
        attended = jnp.einsum('bts,bsd->btd', sparse_probs, x)
        return attended + casimir * 0.01

    def _L0_ffn_ref(x, w1, b1, w2, b2, wr, br):
        import jax, jax.numpy as jnp
        import numpy as np
        B, S, D, H, E, K = (4, 256, 128, 512, 4, 2)
        Bx, Sx, Dx = x.shape
        xf = x.reshape(-1, Dx)
        logits = xf @ wr + br
        topk_vals, topk_idx = jax.lax.top_k(logits, K)
        gates = jax.nn.softmax(topk_vals, axis=-1)
        h = jax.nn.gelu(jnp.einsum('nd,edh->enh', xf, w1) + b1[:, None, :], approximate=False)
        y = jnp.einsum('enh,ehd->end', h, w2) + b2[:, None, :]
        c = jnp.einsum('eh,ehd->ed', jax.nn.gelu(b1, approximate=False), w2) + b2
        c_sum = c.sum(axis=0)
        yt = jnp.transpose(y, (1, 0, 2))
        y_sel = jnp.take_along_axis(yt, topk_idx[:, :, None], axis=1)
        c_sel = c[topk_idx]
        out = jnp.einsum('nk,nkd->nd', gates, y_sel - c_sel + c_sum[None, None, :])
        return out.reshape(Bx, Sx, Dx)
    x = L0_attn_x
    x = x + 0.5 * _L0_ffn_ref(_layernorm(x, axis=-1), L0_ffn_w1, L0_ffn_b1, L0_ffn_w2, L0_ffn_b2, L0_ffn_wr, L0_ffn_br)
    x = x + _L0_attn_ref(_layernorm(x, axis=-1), L0_attn_W)
    x = x + 0.5 * _L0_ffn_ref(_layernorm(x, axis=-1), L0_ffn_w1, L0_ffn_b1, L0_ffn_w2, L0_ffn_b2, L0_ffn_wr, L0_ffn_br)
    return x

_drawn_inputs = setup_inputs


def setup_inputs(seed=0):
    import zlib

    import numpy as np

    out = dict(_drawn_inputs(seed))
    spreads = {}
    factors = {'L0_attn_W': 200.0, 'L0_ffn_br': 2.893}
    for name, (base, spread) in spreads.items():
        noise = np.random.default_rng([zlib.crc32(name.encode()), seed]).standard_normal(out[name].shape)
        drawn = base * np.exp(spread * noise) if base else spread * noise
        out[name] = jnp.asarray(drawn.astype(out[name].dtype))
    for name, factor in factors.items():
        out[name] = (out[name] * factor).astype(out[name].dtype)
    return out
```

```python
from contextlib import ExitStack

import concourse.bass as bass
from concourse import mybir

F32 = mybir.dt.float32
F32R = mybir.dt.float32r
ALU = mybir.AluOpType
ACT = mybir.ActivationFunctionType
AX = mybir.AxisListType

P = 128
TOP_K = 2
THRESH = 0.01
LN_EPS = 1e-5
SUM_EPS = 1e-9
LAG = 3
NBUF = 4
CT = 4


def wait(engine, semaphore, count):
    if not isinstance(count, int) or count > 0:
        engine.wait_ge(semaphore, count)


def build(nc, x, W, w1, b1, w2, b2, wr, br, out):
    B, T, D = x.shape
    E, _, H = w1.shape
    assert D == P and T % (CT * P) == 0 and H % P == 0
    N = B * T
    CH = CT * P
    NCH = N // CH
    NT = N // P
    TB = T // P
    QB = T // CH
    HT = H // P
    K = E * HT
    TILES = NCH * K
    SCALE = float(D) ** -0.5
    assert K % NBUF == 0 and K == 16 and E == 4 and QB == 2 and NCH == 4

    GATE_STEP = [1, 5, 9, 12]
    BACK_STEP = 3
    XT_STEP, LOGIT_STEP, LOGIT_T_STEP, GATE_T_STEP = 6, 9, 11, 15
    ATT_T_STEP = 14
    ROUTER_OPS = 14

    with ExitStack() as ctx:
        def sb(name, shape, dt=F32):
            return ctx.enter_context(nc.sbuf_tensor(name, shape, dt))

        def sem(name):
            return ctx.enter_context(nc.semaphore(name))

        X = sb("X", [P, NT, D])
        w1_raw = sb("w1_raw", [P, E, H])
        w1_hi, w1_lo = sb("w1_hi", [P, E, H], F32R), sb("w1_lo", [P, E, H], F32R)
        w2_raw = sb("w2_raw", [P, K, D])
        w2_hi, w2_lo = sb("w2_hi", [P, K, D], F32R), sb("w2_lo", [P, K, D], F32R)
        W_raw = sb("W_raw", [P, D])
        bias_rows = sb("bias_rows", [K + E, P])
        bias_cols = sb("bias_cols", [P, K + E])
        b1_col, b2_col = bias_cols[:, 0:K], bias_cols[:, K:K + E]
        gelu_b1 = sb("gelu_b1", [P, K])
        wr_raw = sb("wr_raw", [P, E])
        wr_pad = sb("wr_pad", [P, P], F32R)
        br_all = sb("br_all", [P, E])
        ident = sb("ident", [P, P])
        before = sb("before", [P, E, E])
        gate_sel = sb("gate_sel", [2 * E, E, P], F32R)
        c_exp = sb("c_exp", [P, E])
        c_neg = sb("c_neg", [P, E])
        c_sum = sb("c_sum", [P, 1])
        y_shift = sb("y_shift", [P, E])
        w_sum = sb("w_sum", [P, 1])
        w_sum_all = sb("w_sum_all", [P, D])
        eps = sb("eps", [P, CT])
        neg_half = sb("neg_half", [P, CT])

        xT_hi, xT_lo = sb("xT_hi", [P, N], F32R), sb("xT_lo", [P, N], F32R)
        aT_hi, aT_lo = sb("aT_hi", [P, N], F32R), sb("aT_lo", [P, N], F32R)
        aN_hi, aN_lo = sb("aN_hi", [P, NT, D], F32R), sb("aN_lo", [P, NT, D], F32R)

        class Norm:

            def __init__(self, kind):
                self.stats = sb(f"{kind}_stats", [P, CT, 6])
                self.mean_var = sb(f"{kind}_mean_var", [P, CT, 2])
                self.var_eps = sb(f"{kind}_var_eps", [P, CT])
                self.rstd = sb(f"{kind}_rstd", [P, CT])
                self.y = sb(f"{kind}_normed", [P, CT, D])
                self.stats_done = sem(f"{kind}_stats_done")
                self.var_done = sem(f"{kind}_var_done")
                self.eps_done = sem(f"{kind}_eps_done")
                self.rstd_done = sem(f"{kind}_rstd_done")
                self.y_done = sem(f"{kind}_normed_done")

        ffn_norm, att_norm = Norm("ffn"), Norm("att")

        logit_rows = sb("logit_rows", [2 * E, CH])
        logits_lo = sb("logits_lo", [P, CT, E])
        logits = sb("logits", [P, CT, E])
        greater = sb("greater", [P, CT, E, E])
        equal = sb("equal", [P, CT, E, E])
        rank = sb("rank", [P, CT, E])
        taken = sb("taken", [P, CT, E])
        taken_logits = sb("taken_logits", [P, CT, E])
        taken_sum = sb("taken_sum", [P, CT])
        tanh_in = sb("tanh_in", [P, CT, E])
        tanh_out = sb("tanh_out", [P, CT, E])
        gates = sb("gates", [P, CT, E])
        gate_parts = sb("gate_parts", [P, CT, 2 * E])
        gate_rows = sb("gate_rows", [2 * E, CH], F32R)
        gate_all = sb("gate_all", [P, 2, CH])
        h_full = sb("h_full", [P, NBUF, CH])
        h_hi, h_lo = sb("h_hi", [P, NBUF, CH], F32R), sb("h_lo", [P, NBUF, CH], F32R)
        y_sum = sb("y_sum", [P, CH])
        y_gated = sb("y_gated", [P, CH])

        expS = sb("expS", [P, 2, T])
        kept = sb("kept", [P, 2 * CT, T])
        keptT_hi, keptT_lo = sb("keptT_hi", [P, 3, CH], F32R), sb("keptT_lo", [P, 3, CH], F32R)
        Z = sb("Z", [P, NT])
        Z_thresh = sb("Z_thresh", [P, NT])
        kept_sum = sb("kept_sum", [P, NT])
        inv_Z, vac, den, inv_den = (sb(n, [P, CT]) for n in ("inv_Z", "vac", "den", "inv_den"))
        attT = sb("attT", [P, CH])

        h_ps = ctx.enter_context(nc.psum_tensor("h_ps", [P, 4, CH], F32))
        y_ps = ctx.enter_context(nc.psum_tensor("y_ps", [P, 2, CH], F32))
        prep_ps = ctx.enter_context(nc.psum_tensor("prep_ps", [P, CH], F32))
        side_ps = ctx.enter_context(nc.psum_tensor("side_ps", [P, CH], F32))

        x_in = [sem(f"x_in{c}") for c in range(NCH)]
        w1_in = [sem(f"w1_in{e}") for e in range(E)]
        w2_in = [sem(f"w2_in{e}") for e in range(E)]
        bias_in, wr_in, br_in, W_in, out_done = (sem(n) for n in ("bias_in", "wr_in", "br_in", "W_in", "out_done"))
        zeroed, ident_done, before_done, sel_done = (sem(n) for n in ("zeroed", "ident_done", "before_done", "sel_done"))
        wr_zero, wr_hi_done, wr_done, pool_const = (sem(n) for n in ("wr_zero", "wr_hi_done", "wr_done", "pool_const"))
        w1_hi_done, w2_hi_done, w1_lo0_done, w_lo_done = (
            sem(n) for n in ("w1_hi_done", "w2_hi_done", "w1_lo0_done", "w_lo_done"))
        bias_ps, bias_col_done, gelu_b1_done, c_ps, c_step = (
            sem(n) for n in ("bias_ps", "bias_col_done", "gelu_b1_done", "c_ps", "c_step"))
        w_sum_done, w_sum_ps, w_sum_all_done = (sem(n) for n in ("w_sum_done", "w_sum_ps", "w_sum_all_done"))
        xT_ps, xT_hi_done, xT_lo_done = sem("xT_ps"), sem("xT_hi_done"), sem("xT_lo_done")
        logit_ps, logit_rows_done, logitT_ps = sem("logit_ps"), sem("logit_rows_done"), sem("logitT_ps")
        router, tanh_done = sem("router"), sem("tanh_done")
        gateT_ps, gate_rows_done = sem("gateT_ps"), sem("gate_rows_done")
        back_ps, resid_done, y_sum_done = sem("back_ps"), sem("resid_done"), sem("y_sum_done")
        gate_all_ps, gate_all_done, gated = sem("gate_all_ps"), sem("gate_all_done"), sem("gated")
        h_up, h_gelu, h_hi_done, h_lo_done, h_used = (
            sem(n) for n in ("h_up", "h_gelu", "h_hi_done", "h_lo_done", "h_used"))
        aT_ps, aT_hi_done, aT_lo_done, aN_hi_done = (sem(n) for n in ("aT_ps", "aT_hi_done", "aT_lo_done", "aN_hi_done"))
        aN_lo_done = sem("aN_lo_done")
        score_ps, exp_done, thresh_done, kept_done = (sem(n) for n in ("score_ps", "exp_done", "thresh_done", "kept_done"))
        keptT_ps, keptT_hi_done, keptT_lo_done, keptT_used = (
            sem(n) for n in ("keptT_ps", "keptT_hi_done", "keptT_lo_done", "keptT_used"))
        attT_done, att_back, att_small, att_vac, att_out = (
            sem(n) for n in ("attT_done", "att_back", "att_small", "att_vac", "att_out"))

        def chunk_view(t, c):
            b, q = c // QB, c % QB
            return t[b].rearrange("(p i) d -> p i d", p=P)[:, q * CT:(q + 1) * CT, :]

        def chunk(buf, c):
            return buf[:, bass.ds(c * CH, CH)]

        def x_tiles(c):
            return X[:, bass.ds(c * CT, CT), :]

        block = ctx.enter_context(nc.Block())

        @block.sync
        def _(sp):
            def load_w1(e):
                sp.dma_start(w1_raw[:, e, :], w1[e]).then_inc(w1_in[e], 16)

            def load_w2(e):
                sp.dma_start(w2_raw[:, e * HT:(e + 1) * HT, :],
                             w2[e].rearrange("(j p) d -> p j d", p=P)).then_inc(w2_in[e], 16)

            sp.dma_start(x_tiles(0), chunk_view(x, 0)).then_inc(x_in[0], 16)
            load_w1(0)
            sp.dma_start(bias_rows[0:K, :], b1.rearrange("e (j p) -> (e j) p", p=P)).then_inc(bias_in, 16)
            sp.dma_start(bias_rows[K:K + E, :], b2).then_inc(bias_in, 16)
            load_w2(0)
            sp.dma_start(wr_raw[:], wr).then_inc(wr_in, 16)
            sp.dma_start(br_all[:], br.partition_broadcast(P)).then_inc(br_in, 16)
            for e in range(1, E):
                load_w1(e)
                load_w2(e)
                sp.dma_start(x_tiles(e), chunk_view(x, e)).then_inc(x_in[e], 16)
            sp.dma_start(W_raw[:], W).then_inc(W_in, 16)
            for c in range(NCH):
                sp.wait_ge(resid_done, NCH + c + 1)
                sp.dma_start(chunk_view(out, c), x_tiles(c)).then_inc(out_done, 16)
            sp.wait_ge(out_done, 16 * NCH)

        @block.tensor
        def _(pe):
            mm, transpose = nc.tensor.matmul, nc.tensor.transpose

            def three_passes(ps, s_hi, s_lo, m_hi, m_lo, start=True, stop=True):
                mm(ps, s_lo, m_hi, start=start, stop=False)
                mm(ps, s_hi, m_lo, start=False, stop=False)
                return mm(ps, s_hi, m_hi, start=False, stop=stop)

            def up(ph, c, k):
                C = ph * NCH + c
                e, j = k // HT, k % HT
                if k == 0:
                    pe.wait_ge(xT_lo_done, C + 1)
                if isinstance(c, int) and C == 0 and j == 0:
                    pe.wait_ge(w1_hi_done, e + 1)
                    if e == 0:
                        pe.wait_ge(w1_lo0_done, 1)
                    else:
                        pe.wait_ge(w_lo_done, 2 * e)
                wait(pe, h_gelu, C * K + k - NBUF + 1)
                cols = slice(j * P, (j + 1) * P)
                three_passes(h_ps[:, k % NBUF, :], w1_hi[:, e, cols], w1_lo[:, e, cols],
                             chunk(xT_hi, c), chunk(xT_lo, c)).then_inc(h_up, 1)

            def down(ph, c, k):
                C = ph * NCH + c
                e, j = k // HT, k % HT
                if j == 0:
                    wait(pe, gated, C * E + e - 1)
                    if isinstance(c, int) and C == 0:
                        pe.wait_ge(w2_hi_done, e + 1)
                        pe.wait_ge(w_lo_done, 2 * e + 1)
                pe.wait_ge(h_lo_done, C * K + k + 1)
                last = three_passes(y_ps[:, e % 2, :], w2_hi[:, k, :], w2_lo[:, k, :],
                                    h_hi[:, k % NBUF, :], h_lo[:, k % NBUF, :],
                                    start=(j == 0), stop=(j == HT - 1))
                last.then_inc(h_used, 1)

            def normed_T(norm, C, ps, done):
                pe.wait_ge(norm.y_done, C + 1)
                for t in range(CT):
                    last = transpose(ps[:, t * P:(t + 1) * P], norm.y[:, t, :], ident[:])
                last.then_inc(done, 1)

            def x_T(C):
                wait(pe, gate_rows_done, C)
                normed_T(ffn_norm, C, prep_ps, xT_ps)

            def router_logits(c, C):
                pe.wait_ge(xT_lo_done, C + 1)
                if isinstance(C, int) and C == 0:
                    pe.wait_ge(wr_done, 1)
                mm(prep_ps[:], wr_pad[:], chunk(xT_lo, c), start=True, stop=False)
                mm(prep_ps[:], wr_pad[:], chunk(xT_hi, c), start=False, stop=True).then_inc(logit_ps, 1)

            def logits_T(C):
                for t in range(CT):
                    last = transpose(prep_ps[:, t * 2 * E:(t + 1) * 2 * E],
                                     logit_rows[:, t * P:(t + 1) * P], ident[0:2 * E, 0:2 * E])
                last.then_inc(logitT_ps, 1)

            def gates_T(C):
                pe.wait_ge(router, ROUTER_OPS * (C + 1))
                for t in range(CT):
                    last = transpose(prep_ps[0:2 * E, t * P:(t + 1) * P], gate_parts[:, t, :], ident[:])
                last.then_inc(gateT_ps, 1)

            def gate_broadcast(C, e, att_waits):
                if e == 0:
                    pe.wait_ge(gate_rows_done, C + 1)
                    if att_waits is not None:
                        wait(pe, aT_lo_done, att_waits)
                elif e == 1:
                    wait(pe, resid_done, C)
                wait(pe, gate_all_done, C * E + e)
                mm(side_ps[:], gate_sel[:, e, :], gate_rows[:], start=True, stop=True).then_inc(gate_all_ps, 1)

            def back(C, last_of_phase=False):
                pe.wait_ge(y_sum_done, (E - 1) * (C + 1))
                pe.wait_ge(gate_all_done, E * (C + 1) + (0 if last_of_phase else 1))
                for t in range(CT):
                    last = transpose(side_ps[:, t * P:(t + 1) * P], y_sum[:, t * P:(t + 1) * P], ident[:])
                last.then_inc(back_ps, 1)

            def ffn_chunk(ph, c, first=False, last=False):
                C = ph * NCH + c
                for k in range(K):
                    if k == LOGIT_T_STEP and not last:
                        pe.wait_ge(logit_rows_done, C + 2)
                    if k + LAG < K:
                        up(ph, c, k + LAG)
                    elif not last:
                        up(ph, c + 1, k + LAG - K)
                    if k in GATE_STEP:
                        e = GATE_STEP.index(k)
                        gate_broadcast(C, e, (C - 1 if ph == 0 else NCH))
                    if k == BACK_STEP and not first:
                        back(C - 1)
                    if not last:
                        if k == XT_STEP:
                            x_T(C + 1)
                        if k == LOGIT_STEP:
                            router_logits(c + 1, C + 1)
                        if k == LOGIT_T_STEP:
                            logits_T(C + 1)
                    if k == ATT_T_STEP and ph == 0 and not first:
                        pe.wait_ge(gate_all_done, E * (C + 1))
                        normed_T(att_norm, C - 1, side_ps, aT_ps)
                    down(ph, c, k)
                    if k == GATE_T_STEP and not last:
                        gates_T(C + 1)

            def ffn(ph):
                ffn_chunk(ph, 0, first=True)
                with pe.Fori(1, NCH - 1) as c:
                    ffn_chunk(ph, c)
                ffn_chunk(ph, NCH - 1, last=True)

            pe.wait_ge(ident_done, 1)
            pe.wait_ge(bias_in, 32)
            transpose(side_ps[:, 0:K + E], bias_rows[:], ident[0:K + E, 0:K + E]).then_inc(bias_ps, 1)

            x_T(0)
            up(0, 0, 0)
            router_logits(0, 0)
            up(0, 0, 1)
            pe.wait_ge(logit_rows_done, 1)
            logits_T(0)
            up(0, 0, 2)
            pe.wait_ge(gelu_b1_done, 1)
            pe.wait_ge(bias_col_done, 1)
            for e in range(E):
                pe.wait_ge(w2_in[e], 16)
                for j in range(HT):
                    last = mm(side_ps[:, e:e + 1], w2_raw[:, e * HT + j, :], gelu_b1[:, e * HT + j:e * HT + j + 1],
                              start=(j == 0), stop=(j == HT - 1))
            last.then_inc(c_ps, 1)
            gates_T(0)
            pe.wait_ge(c_step, 1)
            ffn(0)

            def scores(s, half):
                b = s // TB
                c = b * QB + half
                if half == 0:
                    wait(pe, exp_done, s - 1)
                    if s % TB == 0:
                        pe.wait_ge(aT_lo_done, (b + 1) * QB)
                tile = slice(s * P, (s + 1) * P)
                last = three_passes(h_ps[:, 2 * (s % 2) + half, :], aT_hi[:, tile], aT_lo[:, tile],
                                    chunk(aT_hi, c), chunk(aT_lo, c))
                if half == QB - 1:
                    last.then_inc(score_ps, 1)

            def kept_T(u):
                q, j = u // TB, u % TB
                if j == 0:
                    pe.wait_ge(kept_done, CT * (q + 1))
                if u == 0:
                    pe.wait_ge(gated, E * NCH)
                wait(pe, keptT_lo_done, u - 1)
                for t in range(CT):
                    last = transpose(y_ps[:, u % 2, t * P:(t + 1) * P],
                                     kept[:, (q * CT + t) % (2 * CT), j * P:(j + 1) * P], ident[:])
                last.then_inc(keptT_ps, 1)

            def attend(u):
                q, j = u // TB, u % TB
                tile = (q // QB) * TB + j
                if j == 0:
                    wait(pe, attT_done, q)
                    if q == 0:
                        pe.wait_ge(resid_done, NCH)
                        pe.wait_ge(aN_lo_done, QB)
                        pe.wait_ge(w_sum_all_done, 1)
                    if q == QB:
                        pe.wait_ge(aN_lo_done, NCH)
                pe.wait_ge(keptT_lo_done, u + 1)
                three_passes(side_ps[:], aN_hi[:, tile, :], aN_lo[:, tile, :],
                             keptT_hi[:, u % 3, :], keptT_lo[:, u % 3, :],
                             start=(j == 0), stop=(j == TB - 1)).then_inc(keptT_used, 1)

            def attend_back(q):
                pe.wait_ge(attT_done, q + 1)
                for t in range(CT):
                    last = transpose(prep_ps[:, t * P:(t + 1) * P], attT[:, t * P:(t + 1) * P], ident[:])
                last.then_inc(att_back, 1)

            for s in range(NT + 7):
                u = 2 * (s - CT - 1)
                if 0 <= u < NCH * TB:
                    kept_T(u)
                if s < NT:
                    scores(s, 0)
                if 0 <= u - 1 < NCH * TB:
                    attend(u - 1)
                if 0 <= u + 1 < NCH * TB:
                    kept_T(u + 1)
                if s < NT:
                    scores(s, 1)
                if 0 <= u < NCH * TB:
                    attend(u)
                if s == 1:
                    back(NCH - 1, last_of_phase=True)
                if s == 3:
                    pe.wait_ge(w_sum_done, 1)
                    pe.wait_ge(resid_done, NCH)
                    mm(side_ps[:, 0:D], w_sum[:].to_broadcast([P, P]), ident[:], start=True,
                       stop=True).then_inc(w_sum_ps, 1)
                if s == 5:
                    normed_T(att_norm, NCH - 1, prep_ps, aT_ps)
                if s >= 10 and (s - 10) % CT == 0 and (s - 10) // CT < NCH:
                    q = (s - 10) // CT
                    if q == 0:
                        pe.wait_ge(aT_lo_done, NCH)
                    if q == 2:
                        pe.wait_ge(router, ROUTER_OPS * NCH + 2)
                    if q == 3:
                        pe.wait_ge(gate_rows_done, NCH + 1)
                    attend_back(q)
                if s == 15:
                    pe.wait_ge(att_out, 2)
                    x_T(NCH)
                if s == 16:
                    router_logits(0, NCH)
                if s == 17:
                    pe.wait_ge(logit_rows_done, NCH + 1)
                    logits_T(NCH)
                if s == 19:
                    pe.wait_ge(att_out, 3)
                    gates_T(NCH)

            pe.wait_ge(exp_done, NT)
            pe.wait_ge(keptT_lo_done, NCH * TB)
            pe.wait_ge(attT_done, NCH)
            for k in range(LAG):
                up(1, 0, k)
            ffn(1)
            back(2 * NCH - 1, last_of_phase=True)

        @block.scalar
        def _(act):
            def copy(dst, src):
                return nc.scalar.activation(dst, src, ACT.Copy)

            def gelu(C, k):
                e = k // HT
                act.wait_ge(h_up, C * K + k + 1)
                wait(act, h_lo_done, C * K + k - NBUF + 1)
                nc.scalar.activation(h_full[:, k % NBUF, :], h_ps[:, k % NBUF, :], ACT.Gelu,
                                     bias=b1_col[:, k:k + 1]).then_inc(h_gelu, 1)

            def hi(C, k):
                act.wait_ge(h_gelu, C * K + k + 1)
                wait(act, h_used, C * K + k - NBUF + 1)
                copy(h_hi[:, k % NBUF, :], h_full[:, k % NBUF, :]).then_inc(h_hi_done, 1)

            def x_hi(c, C):
                act.wait_ge(xT_ps, C + 1)
                copy(chunk(xT_hi, c), prep_ps[:]).then_inc(xT_hi_done, 1)

            def a_hi(c, ps):
                act.wait_ge(aT_ps, c + 1)
                copy(chunk(aT_hi, c), ps[:]).then_inc(aT_hi_done, 1)

            def logit_copy(C):
                act.wait_ge(logit_ps, C + 1)
                copy(logit_rows[:], prep_ps[0:2 * E, :]).then_inc(logit_rows_done, 1)

            def tanh(C):
                act.wait_ge(router, ROUTER_OPS * C + 11)
                nc.scalar.activation(tanh_out[:], tanh_in[:], ACT.Tanh).then_inc(tanh_done, 1)

            def gate_row_copy(C):
                act.wait_ge(gateT_ps, C + 1)
                wait(act, gate_all_ps, E * C)
                copy(gate_rows[:], prep_ps[0:2 * E, :]).then_inc(gate_rows_done, 1)

            def gate_copy(C, e):
                act.wait_ge(gate_all_ps, C * E + e + 1)
                wait(act, gated, C * E + e - 1)
                copy(gate_all[:, e % 2, :], side_ps[:]).then_inc(gate_all_done, 1)

            def w_split_hi(e, w):
                if w == 1:
                    act.wait_ge(w1_in[e], 16)
                    copy(w1_hi[:, e, :], w1_raw[:, e, :]).then_inc(w1_hi_done, 1)
                else:
                    act.wait_ge(w2_in[e], 16)
                    tiles = slice(e * HT, (e + 1) * HT)
                    copy(w2_hi[:, tiles, :], w2_raw[:, tiles, :]).then_inc(w2_hi_done, 1)

            def ffn_chunk(ph, c, first=False, last=False):
                C = ph * NCH + c
                for k in range(K):
                    if k == 0 and not first:
                        gate_row_copy(C)
                    if k - 1 in GATE_STEP:
                        gate_copy(C, GATE_STEP.index(k - 1))
                    if not last:
                        if k == XT_STEP + 1:
                            x_hi(c + 1, C + 1)
                        if k == LOGIT_STEP + 1:
                            logit_copy(C + 1)
                        if k == LOGIT_T_STEP + 2:
                            tanh(C + 1)
                    if k == ATT_T_STEP + 1 and ph == 0 and not first:
                        a_hi(c - 1, side_ps)
                    if k + LAG < K:
                        gelu(C, k + LAG)
                    elif not last:
                        gelu(C + 1, k + LAG - K)
                    if k + LAG - 1 < K:
                        hi(C, k + LAG - 1)
                    elif not last:
                        hi(C + 1, k + LAG - 1 - K)
                    if ph == 0 and first and k in (0, 2, 4, 6, 8):
                        w_split_hi(*[(1, 2), (2, 1), (2, 2), (3, 1), (3, 2)][k // 2])

            def ffn(ph):
                ffn_chunk(ph, 0, first=True)
                with act.Fori(1, NCH - 1) as c:
                    ffn_chunk(ph, c)
                ffn_chunk(ph, NCH - 1, last=True)

            def ffn_start(C):
                gelu(C, 0)
                gelu(C, 1)
                hi(C, 0)
                gelu(C, 2)
                hi(C, 1)

            w_split_hi(0, 1)
            act.wait_ge(bias_ps, 1)
            nc.scalar.activation(gelu_b1[:], side_ps[:, 0:K], ACT.Gelu).then_inc(gelu_b1_done, 1)
            x_hi(0, 0)
            act.wait_ge(bias_col_done, 1)
            gelu(0, 0)
            w_split_hi(0, 2)
            logit_copy(0)
            gelu(0, 1)
            hi(0, 0)
            w_split_hi(1, 1)
            gelu(0, 2)
            hi(0, 1)
            tanh(0)
            gate_row_copy(0)
            ffn(0)

            def exp(s):
                act.wait_ge(score_ps, s + 1)
                wait(act, kept_done, s - 1)
                nc.scalar.activation(expS[:, s % 2, :],
                                     h_ps[:, 2 * (s % 2):2 * (s % 2) + 2, :].rearrange("p a n -> p (a n)"),
                                     ACT.Exp, scale=SCALE, accum_out=Z[:, s:s + 1]).then_inc(exp_done, 1)

            def kept_hi(u):
                act.wait_ge(keptT_ps, u + 1)
                wait(act, keptT_used, u - 2)
                copy(keptT_hi[:, u % 3, :], y_ps[:, u % 2, :]).then_inc(keptT_hi_done, 1)

            for s in range(NT + 7):
                u = 2 * (s - CT - 1)
                for v in (u, u + 1):
                    if 0 <= v < NCH * TB:
                        kept_hi(v)
                if s < NT:
                    exp(s)
                if s >= 9 and (s - 9) % CT == 0 and (s - 9) // CT < NCH:
                    q = (s - 9) // CT
                    act.wait_ge(keptT_used, TB * (q + 1))
                    wait(act, att_back, q)
                    copy(attT[:], side_ps[:]).then_inc(attT_done, 1)
                if s == 6:
                    a_hi(NCH - 1, prep_ps)
                if s == 15:
                    x_hi(0, NCH)
                if s == 16:
                    logit_copy(NCH)
                if s == 18:
                    tanh(NCH)
                if s == 20:
                    gate_row_copy(NCH)
            ffn_start(NCH)
            ffn(1)

        @block.gpsimd
        def _(pool):
            gp = nc.gpsimd

            def rstd(norm, C):
                pool.wait_ge(norm.var_done, C + 1)
                gp.tensor_tensor(norm.var_eps[:], norm.mean_var[:, :, 1], eps[:], ALU.add).then_inc(norm.eps_done, 1)
                pool.wait_ge(norm.eps_done, C + 1)
                gp.tensor_tensor(norm.rstd[:], norm.var_eps[:], neg_half[:], ALU.pow).then_inc(norm.rstd_done, 1)

            def w_split_lo(e, w):
                if w == 1:
                    pool.wait_ge(w1_hi_done, e + 1)
                    gp.tensor_tensor(w1_lo[:, e, :], w1_raw[:, e, :], w1_hi[:, e, :], ALU.subtract).then_inc(w_lo_done, 1)
                else:
                    pool.wait_ge(w2_hi_done, e + 1)
                    tiles = slice(e * HT, (e + 1) * HT)
                    gp.tensor_tensor(w2_lo[:, tiles, :], w2_raw[:, tiles, :], w2_hi[:, tiles, :],
                                     ALU.subtract).then_inc(w_lo_done, 1)

            gp.memset(ident[:], 0.0).then_inc(zeroed, 1)
            gp.memset(neg_half[:], -0.5).then_inc(zeroed, 1)
            gp.memset(eps[:], LN_EPS).then_inc(zeroed, 1)
            pool.wait_ge(zeroed, 3)
            gp.affine_select(out=ident[:], in_=ident[:], compare_op=ALU.not_equal, fill=1.0, base=0,
                             pattern=[[-1, P]], channel_multiplier=1).then_inc(ident_done, 1)
            gp.memset(before[:], 0.0).then_inc(zeroed, 1)
            gp.memset(wr_pad[:].bitcast(F32), 0.0).then_inc(wr_zero, 1)
            rstd(ffn_norm, 0)
            pool.wait_ge(zeroed, 4)
            for e in range(1, E):
                gp.memset(before[:, e, 0:e], 1.0).then_inc(before_done, 1)
            w_split_lo(0, 2)
            w_split_lo(1, 1)
            rstd(ffn_norm, 1)
            for e, w in ((1, 2), (2, 1), (2, 2), (3, 1), (3, 2)):
                w_split_lo(e, w)
            for c in range(NCH):
                if c + 2 < NCH:
                    rstd(ffn_norm, c + 2)
                rstd(att_norm, c)
            with pool.Fori(NCH, 2 * NCH) as C:
                rstd(ffn_norm, C)

        @block.vector
        def _(dve):
            ve = nc.vector

            def norm_stats(norm, c):
                for t in range(CT):
                    last = ve.bn_stats(norm.stats[:, t, :], X[:, c * CT + t, :])
                last.then_inc(norm.stats_done, 1)

            def norm_var(norm):
                for t in range(CT):
                    last = ve.bn_aggr(norm.mean_var[:, t, :], norm.stats[:, t, :])
                last.then_inc(norm.var_done, 1)

            def normalise(norm, c, C):
                dve.wait_ge(norm.rstd_done, C + 1)
                for t in range(CT):
                    last = ve.tensor_scalar(norm.y[:, t, :], X[:, c * CT + t, :], norm.mean_var[:, t, 0:1],
                                            norm.rstd[:, t:t + 1], ALU.subtract, ALU.mult)
                last.then_inc(norm.y_done, 1)

            def x_lo(c, C):
                dve.wait_ge(xT_hi_done, C + 1)
                ve.tensor_tensor(chunk(xT_lo, c), prep_ps[:], chunk(xT_hi, c), ALU.subtract).then_inc(xT_lo_done, 1)

            def a_natural_hi(c):
                dve.wait_ge(att_norm.y_done, c + 1)
                ve.tensor_copy(aN_hi[:, bass.ds(c * CT, CT), :], att_norm.y[:]).then_inc(aN_hi_done, 1)

            def a_natural_lo(c):
                dve.wait_ge(aN_hi_done, c + 1)
                ve.tensor_tensor(aN_lo[:, bass.ds(c * CT, CT), :], att_norm.y[:], aN_hi[:, bass.ds(c * CT, CT), :],
                                 ALU.subtract).then_inc(aN_lo_done, 1)

            def a_lo(c, ps):
                dve.wait_ge(aT_hi_done, c + 1)
                ve.tensor_tensor(chunk(aT_lo, c), ps[:], chunk(aT_hi, c), ALU.subtract).then_inc(aT_lo_done, 1)

            def pairs(a, own):
                return a[:].unsqueeze(3 if own else 2).to_broadcast([P, CT, E, E])

            def router_choice(C):
                dve.wait_ge(logitT_ps, C + 1)
                n = ROUTER_OPS * C
                ps = prep_ps[:, 0:CT * 2 * E].rearrange("p (t e) -> p t e", t=CT)
                ve.tensor_tensor(logits_lo[:], ps[:, :, E:2 * E], br_all[:].unsqueeze(1).to_broadcast([P, CT, E]),
                                 ALU.add).then_inc(router, 1)
                dve.wait_ge(router, n + 1)
                ve.tensor_tensor(logits[:], ps[:, :, 0:E], logits_lo[:], ALU.add).then_inc(router, 1)
                dve.wait_ge(router, n + 2)
                ve.tensor_tensor(greater[:], pairs(logits, False), pairs(logits, True), ALU.is_gt).then_inc(router, 1)
                ve.tensor_tensor(equal[:], pairs(logits, False), pairs(logits, True), ALU.is_equal).then_inc(router, 1)
                dve.wait_ge(router, n + 4)
                for t in range(CT):
                    last = ve.tensor_tensor(equal[:, t], equal[:, t], before[:], ALU.mult)
                last.then_inc(router, 1)
                dve.wait_ge(router, n + 5)
                ve.tensor_tensor(greater[:], greater[:], equal[:], ALU.add).then_inc(router, 1)
                dve.wait_ge(router, n + 6)
                ve.tensor_reduce(rank[:], greater[:], AX.X, ALU.add).then_inc(router, 1)
                dve.wait_ge(router, n + 7)
                ve.tensor_scalar(taken[:], rank[:], TOP_K - 0.5, None, ALU.is_lt).then_inc(router, 1)
                ve.scalar_tensor_tensor(out=taken_logits[:], in0=rank[:], scalar=TOP_K - 0.5, in1=logits[:],
                                        op0=ALU.is_lt, op1=ALU.mult).then_inc(router, 1)
                dve.wait_ge(router, n + 9)
                ve.tensor_reduce(taken_sum[:], taken_logits[:], AX.X, ALU.add).then_inc(router, 1)
                dve.wait_ge(router, n + 10)
                ve.scalar_tensor_tensor(out=tanh_in[:], in0=taken_sum[:].unsqueeze(2).to_broadcast([P, CT, E]),
                                        scalar=-0.5, in1=logits[:], op0=ALU.mult, op1=ALU.add).then_inc(router, 1)

            def router_gates(C):
                dve.wait_ge(tanh_done, C + 1)
                n = ROUTER_OPS * C
                ve.scalar_tensor_tensor(out=gates[:], in0=tanh_out[:], scalar=1.0, in1=taken[:], op0=ALU.add,
                                        op1=ALU.mult).then_inc(router, 1)
                dve.wait_ge(router, n + 12)
                ve.tensor_copy(gate_parts[:, :, 0:E].bitcast(F32R), gates[:]).then_inc(router, 1)
                dve.wait_ge(router, n + 13)
                ve.tensor_tensor(gate_parts[:, :, E:2 * E], gates[:], gate_parts[:, :, 0:E],
                                 ALU.subtract).then_inc(router, 1)

            def lo(C, k):
                dve.wait_ge(h_hi_done, C * K + k + 1)
                wait(dve, h_used, C * K + k - NBUF + 1)
                b = k % NBUF
                ve.tensor_tensor(h_lo[:, b, :], h_full[:, b, :], h_hi[:, b, :], ALU.subtract).then_inc(h_lo_done, 1)

            def gate(C, e):
                dve.wait_ge(h_used, C * K + (e + 1) * HT)
                dve.wait_ge(gate_all_done, C * E + e + 1)
                if e == 0:
                    wait(dve, back_ps, C)
                dst = y_sum if e == 0 else y_gated
                mul = ve.scalar_tensor_tensor(out=dst[:], in0=y_ps[:, e % 2, :], scalar=y_shift[:, e:e + 1],
                                              in1=gate_all[:, e % 2, :], op0=ALU.add, op1=ALU.mult)
                mul.then_inc(gated, 1)
                if e > 0:
                    dve.wait_ge(gated, C * E + e + 1)
                    wait(dve, y_sum_done, C * (E - 1) + e - 1)
                    ve.tensor_tensor(y_sum[:], y_sum[:], y_gated[:], ALU.add).then_inc(y_sum_done, 1)

            def residual(c, C):
                dve.wait_ge(back_ps, C + 1)
                ve.scalar_tensor_tensor(out=x_tiles(c), in0=side_ps[:].rearrange("p (t d) -> p t d", t=CT),
                                        scalar=0.25, in1=x_tiles(c), op0=ALU.mult, op1=ALU.add).then_inc(resid_done, 1)

            def ffn_chunk(ph, c, first=False, last=False):
                C = ph * NCH + c
                att = ph == 0 and not first
                for k in range(K):
                    if k == 0 and not first:
                        gate(C - 1, E - 1)
                    if k == 1 and not last:
                        if first and ph == 0:
                            dve.wait_ge(x_in[1], 16)
                            dve.wait_ge(x_in[2], 16)
                            dve.wait_ge(x_in[3], 16)
                        norm_stats(ffn_norm, c + 1)
                    if k == 4 and not last:
                        wait(dve, xT_ps, C + 1)
                        normalise(ffn_norm, c + 1, C + 1)
                    if k == 4 and not first:
                        residual(c - 1, C - 1)
                    if k > HT and k % HT == 1:
                        gate(C, k // HT - 1)
                    if k == 2 and not last:
                        dve.wait_ge(ffn_norm.stats_done, C + 2)
                    if k == 6 and att:
                        dve.wait_ge(resid_done, C)
                    if k == 7 and att:
                        dve.wait_ge(att_norm.stats_done, C)
                    if k == 8 and not last:
                        x_lo(c + 1, C + 1)
                    if k == 10 and att:
                        wait(dve, aT_ps, C - 1)
                        normalise(att_norm, c - 1, C - 1)
                        a_natural_hi(c - 1)
                    if k == 11 and att:
                        a_natural_lo(c - 1)
                    if k == 12 and not last:
                        router_choice(C + 1)
                    if k == 14 and not last:
                        router_gates(C + 1)
                    if k == 15 and att:
                        a_lo(c - 1, side_ps)
                    if k + LAG - 1 < K:
                        lo(C, k + LAG - 1)
                    elif not last:
                        lo(C + 1, k + LAG - 1 - K)
                    if k == 2 and not last:
                        norm_var(ffn_norm)
                    if k == 6 and att:
                        norm_stats(att_norm, c - 1)
                    if k == 7 and att:
                        norm_var(att_norm)

            def ffn(ph):
                ffn_chunk(ph, 0, first=True)
                with dve.Fori(1, NCH - 1) as c:
                    ffn_chunk(ph, c)
                ffn_chunk(ph, NCH - 1, last=True)

            dve.wait_ge(x_in[0], 16)
            norm_stats(ffn_norm, 0)
            dve.wait_ge(ffn_norm.stats_done, 1)
            norm_var(ffn_norm)
            dve.wait_ge(w1_hi_done, 1)
            ve.tensor_tensor(w1_lo[:, 0, :], w1_raw[:, 0, :], w1_hi[:, 0, :], ALU.subtract).then_inc(w1_lo0_done, 1)
            normalise(ffn_norm, 0, 0)
            dve.wait_ge(gelu_b1_done, 1)
            ve.tensor_copy(bias_cols[:], side_ps[:, 0:K + E]).then_inc(bias_col_done, 1)
            dve.wait_ge(wr_in, 16)
            dve.wait_ge(wr_zero, 1)
            ve.tensor_copy(wr_pad[:, 0:E], wr_raw[:]).then_inc(wr_hi_done, 1)
            dve.wait_ge(wr_hi_done, 1)
            ve.tensor_tensor(wr_pad[:, E:2 * E], wr_raw[:], wr_pad[:, 0:E], ALU.subtract).then_inc(wr_done, 1)
            x_lo(0, 0)
            dve.wait_ge(ident_done, 1)
            for e in range(E):
                last = ve.tensor_tensor(gate_sel[:, e, :], ident[0:2 * E, e:e + 1].to_broadcast([2 * E, P]),
                                        ident[0:2 * E, E + e:E + e + 1].to_broadcast([2 * E, P]), ALU.add)
            last.then_inc(sel_done, 1)
            dve.wait_ge(before_done, E - 1)
            dve.wait_ge(br_in, 16)
            lo(0, 0)
            router_choice(0)
            lo(0, 1)
            router_gates(0)
            dve.wait_ge(c_ps, 1)
            dve.wait_ge(bias_col_done, 1)
            ve.tensor_tensor(c_exp[:], side_ps[:, 0:E], b2_col, ALU.add).then_inc(c_step, 1)
            dve.wait_ge(c_step, 1)
            ve.tensor_reduce(c_sum[:], c_exp[:], AX.X, ALU.add).then_inc(c_step, 1)
            ve.tensor_tensor(c_neg[:], b2_col, c_exp[:], ALU.subtract).then_inc(c_step, 1)
            dve.wait_ge(c_step, 3)
            ve.tensor_scalar(y_shift[:], c_neg[:], c_sum[:], None, ALU.add).then_inc(c_step, 1)
            dve.wait_ge(W_in, 16)
            ve.tensor_reduce(w_sum[:], W_raw[:], AX.X, ALU.add).then_inc(w_sum_done, 1)
            dve.wait_ge(c_step, 4)
            ffn(0)

            def threshold(s):
                dve.wait_ge(exp_done, s + 1)
                ve.tensor_scalar(Z_thresh[:, s:s + 1], Z[:, s:s + 1], THRESH, None, ALU.mult).then_inc(thresh_done, 1)

            def keep(s):
                dve.wait_ge(thresh_done, s + 1)
                q = s // CT
                wait(dve, keptT_ps, TB * (q - 1))
                ve.scalar_tensor_tensor(out=kept[:, s % (2 * CT), :], in0=expS[:, s % 2, :],
                                        scalar=Z_thresh[:, s:s + 1], in1=expS[:, s % 2, :], op0=ALU.is_ge,
                                        op1=ALU.mult, accum_out=kept_sum[:, s:s + 1]).then_inc(kept_done, 1)

            def kept_lo(u):
                dve.wait_ge(keptT_hi_done, u + 1)
                wait(dve, keptT_used, u - 2)
                ve.tensor_tensor(keptT_lo[:, u % 3, :], y_ps[:, u % 2, :], keptT_hi[:, u % 3, :],
                                 ALU.subtract).then_inc(keptT_lo_done, 1)

            def attention_sums(q):
                rows = slice(q * CT, (q + 1) * CT)
                dve.wait_ge(kept_done, CT * (q + 1))
                n = 4 * q
                ve.reciprocal(inv_Z[:], Z[:, rows]).then_inc(att_small, 1)
                ve.tensor_tensor(vac[:], Z[:, rows], kept_sum[:, rows], ALU.subtract).then_inc(att_small, 1)
                ve.scalar_tensor_tensor(out=den[:], in0=Z[:, rows], scalar=SUM_EPS, in1=kept_sum[:, rows],
                                        op0=ALU.mult, op1=ALU.add).then_inc(att_small, 1)
                dve.wait_ge(att_small, n + 3)
                ve.tensor_tensor(vac[:], vac[:], inv_Z[:], ALU.mult)
                ve.reciprocal(inv_den[:], den[:]).then_inc(att_small, 1)
                dve.wait_ge(att_small, n + 4)

            def attention_out(q):
                for t in range(CT):
                    xt = X[:, q * CT + t, :]
                    last = ve.scalar_tensor_tensor(out=xt, in0=w_sum_all[:], scalar=vac[:, t:t + 1], in1=xt,
                                                   op0=ALU.mult, op1=ALU.add)
                last.then_inc(att_vac, 1)
                dve.wait_ge(att_vac, q + 1)
                dve.wait_ge(att_back, q + 1)
                for t in range(CT):
                    xt = X[:, q * CT + t, :]
                    last = ve.scalar_tensor_tensor(out=xt, in0=prep_ps[:, t * P:(t + 1) * P], scalar=inv_den[:, t:t + 1],
                                                   in1=xt, op0=ALU.mult, op1=ALU.add)
                last.then_inc(att_out, 1)

            for s in range(NT + 7):
                u = 2 * (s - CT - 1)
                if s == 0:
                    gate(NCH - 1, E - 1)
                if s == 2:
                    residual(NCH - 1, NCH - 1)
                    dve.wait_ge(resid_done, NCH)
                    norm_stats(att_norm, NCH - 1)
                    dve.wait_ge(att_norm.stats_done, NCH)
                    norm_var(att_norm)
                if s == 4:
                    dve.wait_ge(aT_ps, NCH - 1)
                    normalise(att_norm, NCH - 1, NCH - 1)
                    a_natural_hi(NCH - 1)
                    a_natural_lo(NCH - 1)
                    dve.wait_ge(w_sum_ps, 1)
                    ve.tensor_scalar(w_sum_all[:], side_ps[:, 0:D], 0.01, None, ALU.mult).then_inc(w_sum_all_done, 1)
                if 1 <= s <= NT:
                    threshold(s - 1)
                if 0 <= u < NCH * TB:
                    kept_lo(u)
                if 1 <= s <= NT:
                    keep(s - 1)
                if 0 <= u + 1 < NCH * TB:
                    kept_lo(u + 1)
                if s == 6:
                    a_lo(NCH - 1, prep_ps)
                if s == 11:
                    dve.wait_ge(att_out, 1)
                    norm_stats(ffn_norm, 0)
                    dve.wait_ge(ffn_norm.stats_done, NCH + 1)
                    norm_var(ffn_norm)
                if s == 13:
                    dve.wait_ge(xT_ps, NCH)
                    normalise(ffn_norm, 0, NCH)
                if s == 16:
                    x_lo(0, NCH)
                if s == 18:
                    router_choice(NCH)
                if s == 19:
                    router_gates(NCH)
                if s >= 10 and (s - 10) % CT == 0 and (s - 10) // CT < NCH:
                    q = (s - 10) // CT
                    attention_sums(q)
                    attention_out(q)
            dve.wait_ge(att_out, NCH)
            lo(NCH, 0)
            lo(NCH, 1)
            ffn(1)
            gate(2 * NCH - 1, E - 1)
            residual(NCH - 1, 2 * NCH - 1)


_INS = ['L0_attn_x', 'L0_attn_W', 'L0_ffn_w1', 'L0_ffn_b1', 'L0_ffn_w2', 'L0_ffn_b2', 'L0_ffn_wr', 'L0_ffn_br']


def kernel(**inputs):
    import numpy as _np
    import concourse.bacc as _bacc
    from concourse import mybir as _mybir
    from concourse.bass_utils import run_bass_kernel_spmd as _run

    nc = _bacc.Bacc("TRN2", target_bir_lowering=False, num_devices=1)
    arrays, args = {}, []
    for name in _INS:
        a = _np.ascontiguousarray(inputs[name])
        arrays[f"in_{name}"] = a
        args.append(nc.dram_tensor(f"in_{name}", a.shape, _mybir.dt.from_np(a.dtype), kind="ExternalInput").ap())
    shape = inputs['L0_attn_x'].shape
    args.append(nc.dram_tensor("out_0", shape, _mybir.dt.float32, kind="ExternalOutput").ap())
    build(nc, *args)
    r = _run(nc, [arrays], core_ids=[0])
    return r.results[0]["out_0"]
```

```python
from contextlib import ExitStack

import concourse.bass as bass
from concourse import mybir

F32 = mybir.dt.float32
F32R = mybir.dt.float32r
ALU = mybir.AluOpType
ACT = mybir.ActivationFunctionType
AX = mybir.AxisListType

P = 128
TOP_K = 2
THRESH = 0.01
LN_EPS = 1e-5
SUM_EPS = 1e-9
LAG = 3
NBUF = 4
CT = 4


def wait(engine, semaphore, count):
    if not isinstance(count, int) or count > 0:
        engine.wait_ge(semaphore, count)


def build(nc, x, W, w1, b1, w2, b2, wr, br, out):
    B, T, D = x.shape
    E, _, H = w1.shape
    assert D == P and T % (CT * P) == 0 and H % P == 0
    N = B * T
    CH = CT * P
    NCH = N // CH
    NT = N // P
    TB = T // P
    QB = T // CH
    HT = H // P
    K = E * HT
    TILES = NCH * K
    SCALE = float(D) ** -0.5
    assert K % NBUF == 0 and K == 16 and E == 4 and QB == 2 and NCH == 4

    GATE_STEP = [3, 7, 10, 12]
    BACK_STEP = 5
    XT_STEP, LOGIT_STEP, LOGIT_T_STEP = 7, 10, 12
    GATE_T_STEP = 1
    EARLY_STEP = [13, 15]
    EARLY = len(EARLY_STEP)
    NEXP = 3
    ATT_T_STEP = 14
    ROUTER_OPS = 14

    with ExitStack() as ctx:
        def sb(name, shape, dt=F32):
            return ctx.enter_context(nc.sbuf_tensor(name, shape, dt))

        def sem(name):
            return ctx.enter_context(nc.semaphore(name))

        X = sb("X", [P, NT, D])
        w1_raw = sb("w1_raw", [P, E, H])
        w1_hi, w1_lo = sb("w1_hi", [P, E, H], F32R), sb("w1_lo", [P, E, H], F32R)
        w2_raw = sb("w2_raw", [P, K, D])
        w2_hi, w2_lo = sb("w2_hi", [P, K, D], F32R), sb("w2_lo", [P, K, D], F32R)
        W_raw = sb("W_raw", [P, D])
        bias_rows = sb("bias_rows", [K + E, P])
        bias_cols = sb("bias_cols", [P, K + E])
        b1_col, b2_col = bias_cols[:, 0:K], bias_cols[:, K:K + E]
        gelu_b1 = sb("gelu_b1", [P, K])
        wr_raw = sb("wr_raw", [P, E])
        wr_pad = sb("wr_pad", [P, P], F32R)
        br_all = sb("br_all", [P, E])
        ident = sb("ident", [P, P])
        before = sb("before", [P, E, E])
        gate_sel = sb("gate_sel", [2 * E, E, P], F32R)
        c_row = sb("c_row", [1, E * D])
        c_exp = sb("c_exp", [P, E])
        c_neg = sb("c_neg", [P, E])
        c_sum = sb("c_sum", [P, 1])
        y_shift = sb("y_shift", [P, E])
        w_sum = sb("w_sum", [P, 1])
        w_sum_all = sb("w_sum_all", [P, D])
        eps = sb("eps", [P, CT])
        neg_half = sb("neg_half", [P, CT])

        xT_hi, xT_lo = sb("xT_hi", [P, N], F32R), sb("xT_lo", [P, N], F32R)
        aT_hi, aT_lo = sb("aT_hi", [P, N], F32R), sb("aT_lo", [P, N], F32R)
        aN_hi, aN_lo = sb("aN_hi", [P, NT, D], F32R), sb("aN_lo", [P, NT, D], F32R)

        class Norm:

            def __init__(self, kind):
                self.stats = sb(f"{kind}_stats", [P, CT, 6])
                self.mean_var = sb(f"{kind}_mean_var", [P, CT, 2])
                self.var_eps = sb(f"{kind}_var_eps", [P, CT])
                self.rstd = sb(f"{kind}_rstd", [P, CT])
                self.y = sb(f"{kind}_normed", [P, CT, D])
                self.stats_done = sem(f"{kind}_stats_done")
                self.var_done = sem(f"{kind}_var_done")
                self.eps_done = sem(f"{kind}_eps_done")
                self.rstd_done = sem(f"{kind}_rstd_done")
                self.y_done = sem(f"{kind}_normed_done")

        ffn_norm, att_norm = Norm("ffn"), Norm("att")

        logit_rows = sb("logit_rows", [2 * E, CH])
        logits_lo = sb("logits_lo", [P, CT, E])
        logits = sb("logits", [P, CT, E])
        greater = sb("greater", [P, CT, E, E])
        equal = sb("equal", [P, CT, E, E])
        rank = sb("rank", [P, CT, E])
        taken = sb("taken", [P, CT, E])
        taken_logits = sb("taken_logits", [P, CT, E])
        taken_sum = sb("taken_sum", [P, CT])
        tanh_in = sb("tanh_in", [P, CT, E])
        tanh_out = sb("tanh_out", [P, CT, E])
        gates = sb("gates", [P, CT, E])
        gate_parts = sb("gate_parts", [P, CT, 2 * E])
        gate_rows = sb("gate_rows", [2 * E, CH], F32R)
        gate_all = sb("gate_all", [P, 2, CH])
        h_full = sb("h_full", [P, NBUF, CH])
        h_hi, h_lo = sb("h_hi", [P, NBUF, CH], F32R), sb("h_lo", [P, NBUF, CH], F32R)
        y_sum = sb("y_sum", [P, CH])
        y_gated = sb("y_gated", [P, 2, CH])

        expS = sb("expS", [P, NEXP, T])
        kept = sb("kept", [P, 2 * CT, T])
        keptT_hi, keptT_lo = h_hi, h_lo
        Z = sb("Z", [P, NT])
        Z_thresh = sb("Z_thresh", [P, NT])
        kept_sum = sb("kept_sum", [P, NT])
        inv_Z, vac, den, inv_den = (sb(n, [P, CT]) for n in ("inv_Z", "vac", "den", "inv_den"))
        attT = sb("attT", [P, CH])

        h_ps = ctx.enter_context(nc.psum_tensor("h_ps", [P, 4, CH], F32))
        y_ps = ctx.enter_context(nc.psum_tensor("y_ps", [P, 2, CH], F32))
        prep_ps = ctx.enter_context(nc.psum_tensor("prep_ps", [P, CH], F32))
        side_ps = ctx.enter_context(nc.psum_tensor("side_ps", [P, CH], F32))

        x_in = [sem(f"x_in{c}") for c in range(NCH)]
        w1_in = [sem(f"w1_in{e}") for e in range(E)]
        w2_in = [sem(f"w2_in{e}") for e in range(E)]
        bias_in, wr_in, br_in, W_in, out_done = (sem(n) for n in ("bias_in", "wr_in", "br_in", "W_in", "out_done"))
        zeroed, ident_done, before_done, sel_done = (sem(n) for n in ("zeroed", "ident_done", "before_done", "sel_done"))
        wr_zero, wr_hi_done, wr_done, pool_const = (sem(n) for n in ("wr_zero", "wr_hi_done", "wr_done", "pool_const"))
        w1_hi_done, w2_hi_done, w1_lo0_done, w_lo_done = (
            sem(n) for n in ("w1_hi_done", "w2_hi_done", "w1_lo0_done", "w_lo_done"))
        bias_ps, bias_col_done, gelu_b1_done, c_row_ps, c_row_done, c_ps, c_step = (
            sem(n) for n in ("bias_ps", "bias_col_done", "gelu_b1_done", "c_row_ps", "c_row_done", "c_ps", "c_step"))
        w_sum_done, w_sum_ps, w_sum_all_done = (sem(n) for n in ("w_sum_done", "w_sum_ps", "w_sum_all_done"))
        xT_ps, xT_hi_done, xT_lo_done = sem("xT_ps"), sem("xT_hi_done"), sem("xT_lo_done")
        logit_ps, logit_rows_done, logitT_ps = sem("logit_ps"), sem("logit_rows_done"), sem("logitT_ps")
        router, tanh_done = sem("router"), sem("tanh_done")
        gateT_ps, gate_rows_done = sem("gateT_ps"), sem("gate_rows_done")
        back_ps, resid_done, y_sum_done = sem("back_ps"), sem("resid_done"), sem("y_sum_done")
        gate_all_ps, gate_all_done, gated = sem("gate_all_ps"), sem("gate_all_done"), sem("gated")
        h_up, h_gelu, h_lo_done, h_used = (
            sem(n) for n in ("h_up", "h_gelu", "h_lo_done", "h_used"))
        aT_ps, aT_hi_done, aT_lo_done, aN_hi_done = (sem(n) for n in ("aT_ps", "aT_hi_done", "aT_lo_done", "aN_hi_done"))
        aN_lo_done = sem("aN_lo_done")
        score_ps, exp_done, thresh_done, kept_done = (sem(n) for n in ("score_ps", "exp_done", "thresh_done", "kept_done"))
        keptT_ps, keptT_hi_done, keptT_lo_done, keptT_used = (
            sem(n) for n in ("keptT_ps", "keptT_hi_done", "keptT_lo_done", "keptT_used"))
        attT_done, att_back, att_small, att_vac, att_out = (
            sem(n) for n in ("attT_done", "att_back", "att_small", "att_vac", "att_out"))

        def chunk_view(t, c):
            b, q = c // QB, c % QB
            return t[b].rearrange("(p i) d -> p i d", p=P)[:, q * CT:(q + 1) * CT, :]

        def chunk(buf, c):
            return buf[:, bass.ds(c * CH, CH)]

        def x_tiles(c):
            return X[:, bass.ds(c * CT, CT), :]

        block = ctx.enter_context(nc.Block())

        @block.sync
        def _(sp):
            def load_w1(e):
                sp.dma_start(w1_raw[:, e, :], w1[e]).then_inc(w1_in[e], 16)

            def load_w2(e):
                sp.dma_start(w2_raw[:, e * HT:(e + 1) * HT, :],
                             w2[e].rearrange("(j p) d -> p j d", p=P)).then_inc(w2_in[e], 16)

            sp.dma_start(x_tiles(0), chunk_view(x, 0)).then_inc(x_in[0], 16)
            load_w1(0)
            sp.dma_start(bias_rows[0:K, :], b1.rearrange("e (j p) -> (e j) p", p=P)).then_inc(bias_in, 16)
            sp.dma_start(bias_rows[K:K + E, :], b2).then_inc(bias_in, 16)
            load_w2(0)
            sp.dma_start(wr_raw[:], wr).then_inc(wr_in, 16)
            sp.dma_start(br_all[:], br.partition_broadcast(P)).then_inc(br_in, 16)
            for e in range(1, E):
                load_w1(e)
                load_w2(e)
                sp.dma_start(x_tiles(e), chunk_view(x, e)).then_inc(x_in[e], 16)
            sp.dma_start(W_raw[:], W).then_inc(W_in, 16)
            for c in range(NCH):
                sp.wait_ge(resid_done, NCH + c + 1)
                sp.dma_start(chunk_view(out, c), x_tiles(c)).then_inc(out_done, 16)
            sp.wait_ge(out_done, 16 * NCH)

        @block.tensor
        def _(pe):
            mm, transpose = nc.tensor.matmul, nc.tensor.transpose

            def three_passes(ps, s_hi, s_lo, m_hi, m_lo, start=True, stop=True):
                mm(ps, s_lo, m_hi, start=start, stop=False)
                mm(ps, s_hi, m_lo, start=False, stop=False)
                return mm(ps, s_hi, m_hi, start=False, stop=stop)

            def up(ph, c, k):
                C = ph * NCH + c
                e, j = k // HT, k % HT
                if k == 0:
                    pe.wait_ge(xT_lo_done, C + 1)
                if isinstance(c, int) and C == 0 and j == 0:
                    pe.wait_ge(w1_hi_done, e + 1)
                    if e == 0:
                        pe.wait_ge(w1_lo0_done, 1)
                    else:
                        pe.wait_ge(w_lo_done, 2 * e)
                wait(pe, h_gelu, C * K + k - NBUF + 1)
                cols = slice(j * P, (j + 1) * P)
                three_passes(h_ps[:, k % NBUF, :], w1_hi[:, e, cols], w1_lo[:, e, cols],
                             chunk(xT_hi, c), chunk(xT_lo, c)).then_inc(h_up, 1)

            def down(ph, c, k):
                C = ph * NCH + c
                e, j = k // HT, k % HT
                if j == 0:
                    wait(pe, gated, C * E + e - 1)
                    if isinstance(c, int) and C == 0:
                        pe.wait_ge(w2_hi_done, e + 1)
                        pe.wait_ge(w_lo_done, 2 * e + 1)
                pe.wait_ge(h_lo_done, C * K + k + 1)
                last = three_passes(y_ps[:, e % 2, :], w2_hi[:, k, :], w2_lo[:, k, :],
                                    h_hi[:, k % NBUF, :], h_lo[:, k % NBUF, :],
                                    start=(j == 0), stop=(j == HT - 1))
                last.then_inc(h_used, 1)

            def normed_T(norm, C, ps, done):
                pe.wait_ge(norm.y_done, C + 1)
                for t in range(CT):
                    last = transpose(ps[:, t * P:(t + 1) * P], norm.y[:, t, :], ident[:])
                last.then_inc(done, 1)

            def x_T(C):
                wait(pe, gate_rows_done, C)
                normed_T(ffn_norm, C, prep_ps, xT_ps)

            def router_logits(c, C):
                pe.wait_ge(xT_lo_done, C + 1)
                if isinstance(C, int) and C == 0:
                    pe.wait_ge(wr_done, 1)
                mm(prep_ps[:], wr_pad[:], chunk(xT_lo, c), start=True, stop=False)
                mm(prep_ps[:], wr_pad[:], chunk(xT_hi, c), start=False, stop=True).then_inc(logit_ps, 1)

            def logits_T(C):
                for t in range(CT):
                    last = transpose(prep_ps[:, t * 2 * E:(t + 1) * 2 * E],
                                     logit_rows[:, t * P:(t + 1) * P], ident[0:2 * E, 0:2 * E])
                last.then_inc(logitT_ps, 1)

            def gates_T(C):
                pe.wait_ge(router, ROUTER_OPS * (C + 1))
                for t in range(CT):
                    last = transpose(prep_ps[0:2 * E, t * P:(t + 1) * P], gate_parts[:, t, :], ident[:])
                last.then_inc(gateT_ps, 1)

            def gate_broadcast(C, e, att_waits):
                if e == 0:
                    pe.wait_ge(gate_rows_done, C + 1)
                    if att_waits is not None:
                        wait(pe, aT_lo_done, att_waits)
                elif e == 1 and isinstance(C, int) and C == 0:
                    pe.wait_ge(w_sum_all_done, 1)
                elif e == 1:
                    wait(pe, resid_done, C)
                wait(pe, gate_all_done, C * E + e)
                mm(side_ps[:], gate_sel[:, e, :], gate_rows[:], start=True, stop=True).then_inc(gate_all_ps, 1)

            def back(C, last_of_phase=False):
                pe.wait_ge(y_sum_done, (E - 1) * (C + 1))
                pe.wait_ge(gate_all_done, E * (C + 1) + (0 if last_of_phase else 1))
                for t in range(CT):
                    last = transpose(side_ps[:, t * P:(t + 1) * P], y_sum[:, t * P:(t + 1) * P], ident[:])
                last.then_inc(back_ps, 1)

            def scores(s, half):
                b = s // TB
                c = b * QB + half
                if half == 0:
                    if s < EARLY:
                        pe.wait_ge(h_gelu, (NCH - 1) * K + K - NBUF + 2 * s + 2)
                    wait(pe, exp_done, s - 1)
                    if s % TB == 0:
                        pe.wait_ge(aT_lo_done, (b + 1) * QB)
                tile = slice(s * P, (s + 1) * P)
                last = three_passes(h_ps[:, 2 * (s % 2) + half, :], aT_hi[:, tile], aT_lo[:, tile],
                                    chunk(aT_hi, c), chunk(aT_lo, c))
                if half == QB - 1:
                    last.then_inc(score_ps, 1)

            def ffn_chunk(ph, c, first=False, last=False):
                C = ph * NCH + c
                for k in range(K):
                    if k == LOGIT_T_STEP and not last:
                        pe.wait_ge(logit_rows_done, C + 2)
                    if k + LAG < K:
                        up(ph, c, k + LAG)
                    elif not last:
                        up(ph, c + 1, k + LAG - K)
                    if k in GATE_STEP:
                        e = GATE_STEP.index(k)
                        gate_broadcast(C, e, (C - 1 if ph == 0 else NCH))
                    if k == BACK_STEP and not first:
                        back(C - 1)
                    if k == BACK_STEP and first and ph == 0:
                        pe.wait_ge(w_sum_done, 1)
                        pe.wait_ge(gate_all_done, 1)
                        mm(side_ps[:, 0:D], w_sum[:].to_broadcast([P, P]), ident[:], start=True,
                           stop=True).then_inc(w_sum_ps, 1)
                    if not last:
                        if k == XT_STEP:
                            x_T(C + 1)
                        if k == LOGIT_STEP:
                            router_logits(c + 1, C + 1)
                        if k == LOGIT_T_STEP:
                            logits_T(C + 1)
                    if k == ATT_T_STEP and ph == 0 and not first:
                        pe.wait_ge(gate_all_done, E * (C + 1))
                        normed_T(att_norm, C - 1, side_ps, aT_ps)
                    if ph == 0 and last and k in EARLY_STEP:
                        scores(EARLY_STEP.index(k), 0)
                        scores(EARLY_STEP.index(k), 1)
                    down(ph, c, k)
                    if k == GATE_T_STEP:
                        if ph == 1 and first:
                            pe.wait_ge(att_out, NCH)
                        gates_T(C)

            def ffn(ph):
                ffn_chunk(ph, 0, first=True)
                with pe.Fori(1, NCH - 1) as c:
                    ffn_chunk(ph, c)
                ffn_chunk(ph, NCH - 1, last=True)

            pe.wait_ge(ident_done, 1)
            pe.wait_ge(bias_in, 32)
            transpose(side_ps[:, 0:K + E], bias_rows[:], ident[0:K + E, 0:K + E]).then_inc(bias_ps, 1)

            x_T(0)
            up(0, 0, 0)
            router_logits(0, 0)
            up(0, 0, 1)
            pe.wait_ge(logit_rows_done, 1)
            logits_T(0)
            pe.wait_ge(gelu_b1_done, 1)
            pe.wait_ge(bias_col_done, 1)
            for e in range(E):
                pe.wait_ge(w2_in[e], 16)
                for j in range(HT):
                    last = mm(side_ps[0:1, e * D:(e + 1) * D], gelu_b1[:, e * HT + j:e * HT + j + 1],
                              w2_raw[:, e * HT + j, :], start=(j == 0), stop=(j == HT - 1))
            last.then_inc(c_row_ps, 1)
            up(0, 0, 2)
            pe.wait_ge(c_row_done, 1)
            for e in range(E):
                last = transpose(side_ps[:, e:e + 1], c_row[:, e * D:(e + 1) * D], ident[0:1, 0:1])
            last.then_inc(c_ps, 1)
            pe.wait_ge(c_step, 1)
            ffn(0)

            def kept_T(u):
                q, j = u // TB, u % TB
                if j == 0:
                    pe.wait_ge(kept_done, CT * (q + 1))
                if u == 0:
                    pe.wait_ge(gated, E * NCH)
                wait(pe, keptT_lo_done, u - 1)
                for t in range(CT):
                    last = transpose(y_ps[:, u % 2, t * P:(t + 1) * P],
                                     kept[:, (q * CT + t) % (2 * CT), j * P:(j + 1) * P], ident[:])
                last.then_inc(keptT_ps, 1)

            def att_ps(q):
                return (side_ps, prep_ps)[q % 2]

            def attend(u):
                q, j = u // TB, u % TB
                tile = (q // QB) * TB + j
                if j == 0:
                    wait(pe, att_out, q - 1)
                    if q == 0:
                        pe.wait_ge(resid_done, NCH)
                        pe.wait_ge(aN_lo_done, QB)
                    if q == 1:
                        pe.wait_ge(aT_lo_done, NCH)
                    if q == QB:
                        pe.wait_ge(aN_lo_done, NCH)
                    if q == NCH - 1:
                        pe.wait_ge(router, ROUTER_OPS * NCH + 2)
                pe.wait_ge(keptT_lo_done, u + 1)
                three_passes(att_ps(q)[:], aN_hi[:, tile, :], aN_lo[:, tile, :],
                             keptT_hi[:, u % NBUF, :], keptT_lo[:, u % NBUF, :],
                             start=(j == 0), stop=(j == TB - 1)).then_inc(keptT_used, 1)

            def attend_back(q):
                pe.wait_ge(attT_done, q + 1)
                for t in range(CT):
                    last = transpose(att_ps(q)[:, t * P:(t + 1) * P], attT[:, t * P:(t + 1) * P], ident[:])
                last.then_inc(att_back, 1)

            for s in range(EARLY, NT + 7):
                u = 2 * (s - CT - 1)
                if 0 <= u < NCH * TB:
                    kept_T(u)
                if s < NT:
                    scores(s, 0)
                if 0 <= u - 2 < NCH * TB:
                    attend(u - 2)
                if 0 <= u + 1 < NCH * TB:
                    kept_T(u + 1)
                if s < NT:
                    scores(s, 1)
                if 0 <= u - 1 < NCH * TB:
                    attend(u - 1)
                if s == 3:
                    back(NCH - 1, last_of_phase=True)
                if s == 6:
                    normed_T(att_norm, NCH - 1, prep_ps, aT_ps)
                if s >= 10 and (s - 10) % CT == 0 and (s - 10) // CT < NCH:
                    q = (s - 10) // CT
                    attend_back(q)
                if s == 15:
                    pe.wait_ge(att_out, 2)
                    x_T(NCH)
                if s == 16:
                    router_logits(0, NCH)
                if s == 17:
                    pe.wait_ge(logit_rows_done, NCH + 1)
                    logits_T(NCH)

            pe.wait_ge(exp_done, NT)
            pe.wait_ge(keptT_lo_done, NCH * TB)
            pe.wait_ge(attT_done, NCH)
            for k in range(LAG):
                up(1, 0, k)
            ffn(1)
            back(2 * NCH - 1, last_of_phase=True)

        @block.scalar
        def _(act):
            def copy(dst, src):
                return nc.scalar.activation(dst, src, ACT.Copy)

            def gelu(C, k):
                act.wait_ge(h_up, C * K + k + 1)
                wait(act, h_lo_done, C * K + k - NBUF + 1)
                nc.scalar.activation(h_full[:, k % NBUF, :], h_ps[:, k % NBUF, :], ACT.Gelu, bias=b1_col[:, k:k + 1])
                wait(act, h_used, C * K + k - NBUF + 1)
                nc.scalar.activation(h_hi[:, k % NBUF, :], h_ps[:, k % NBUF, :], ACT.Gelu,
                                     bias=b1_col[:, k:k + 1]).then_inc(h_gelu, 1)

            def x_hi(c, C):
                act.wait_ge(xT_ps, C + 1)
                copy(chunk(xT_hi, c), prep_ps[:]).then_inc(xT_hi_done, 1)

            def a_hi(c, ps):
                act.wait_ge(aT_ps, c + 1)
                copy(chunk(aT_hi, c), ps[:]).then_inc(aT_hi_done, 1)

            def logit_copy(C):
                act.wait_ge(logit_ps, C + 1)
                copy(logit_rows[:], prep_ps[0:2 * E, :]).then_inc(logit_rows_done, 1)

            def tanh(C):
                act.wait_ge(router, ROUTER_OPS * C + 11)
                nc.scalar.activation(tanh_out[:], tanh_in[:], ACT.Tanh).then_inc(tanh_done, 1)

            def gate_row_copy(C):
                act.wait_ge(gateT_ps, C + 1)
                wait(act, gate_all_ps, E * C)
                copy(gate_rows[:], prep_ps[0:2 * E, :]).then_inc(gate_rows_done, 1)

            def gate_copy(C, e):
                act.wait_ge(gate_all_ps, C * E + e + 1)
                wait(act, gated, C * E + e - 1)
                copy(gate_all[:, e % 2, :], side_ps[:]).then_inc(gate_all_done, 1)

            def w_split_hi(e, w):
                if w == 1:
                    act.wait_ge(w1_in[e], 16)
                    copy(w1_hi[:, e, :], w1_raw[:, e, :]).then_inc(w1_hi_done, 1)
                else:
                    act.wait_ge(w2_in[e], 16)
                    tiles = slice(e * HT, (e + 1) * HT)
                    copy(w2_hi[:, tiles, :], w2_raw[:, tiles, :]).then_inc(w2_hi_done, 1)

            def exp(s):
                act.wait_ge(score_ps, s + 1)
                wait(act, kept_done, s - NEXP + 1)
                nc.scalar.activation(expS[:, s % NEXP, :],
                                     h_ps[:, 2 * (s % 2):2 * (s % 2) + 2, :].rearrange("p a n -> p (a n)"),
                                     ACT.Exp, scale=SCALE, accum_out=Z[:, s:s + 1]).then_inc(exp_done, 1)

            def ffn_chunk(ph, c, first=False, last=False):
                C = ph * NCH + c
                for k in range(K):
                    if k == GATE_T_STEP + 1:
                        gate_row_copy(C)
                    if k - 1 in GATE_STEP:
                        gate_copy(C, GATE_STEP.index(k - 1))
                    if not last:
                        if k == XT_STEP + 1:
                            x_hi(c + 1, C + 1)
                        if k == LOGIT_STEP + 1:
                            logit_copy(C + 1)
                    if k == ATT_T_STEP + 1 and ph == 0 and not first:
                        a_hi(c - 1, side_ps)
                    if ph == 0 and last and k - 1 in EARLY_STEP:
                        exp(EARLY_STEP.index(k - 1))
                    if k + LAG < K:
                        gelu(C, k + LAG)
                    elif not last:
                        gelu(C + 1, k + LAG - K)
                    if k == LOGIT_T_STEP + 3 and not last:
                        tanh(C + 1)
                    if ph == 0 and first and k in (0, 2, 4, 6, 8):
                        w_split_hi(*[(1, 2), (2, 1), (2, 2), (3, 1), (3, 2)][k // 2])

            def ffn(ph):
                ffn_chunk(ph, 0, first=True)
                with act.Fori(1, NCH - 1) as c:
                    ffn_chunk(ph, c)
                ffn_chunk(ph, NCH - 1, last=True)

            def ffn_start(C):
                for k in range(LAG):
                    gelu(C, k)

            w_split_hi(0, 1)
            act.wait_ge(bias_ps, 1)
            nc.scalar.activation(gelu_b1[:], side_ps[:, 0:K], ACT.Gelu).then_inc(gelu_b1_done, 1)
            x_hi(0, 0)
            act.wait_ge(bias_col_done, 1)
            gelu(0, 0)
            w_split_hi(0, 2)
            logit_copy(0)
            gelu(0, 1)
            w_split_hi(1, 1)
            act.wait_ge(c_row_ps, 1)
            copy(c_row[:], side_ps[0:1, :]).then_inc(c_row_done, 1)
            gelu(0, 2)
            tanh(0)
            ffn(0)

            def kept_hi(u):
                act.wait_ge(keptT_ps, u + 1)
                wait(act, keptT_used, u - NBUF + 1)
                copy(keptT_hi[:, u % NBUF, :], y_ps[:, u % 2, :]).then_inc(keptT_hi_done, 1)

            for s in range(EARLY, NT + 7):
                u = 2 * (s - CT - 1)
                if s == EARLY:
                    exp(EARLY - 1)
                if s == 7:
                    a_hi(NCH - 1, prep_ps)
                if 0 <= u < NCH * TB:
                    kept_hi(u)
                if s >= 10 and (s - 10) % CT == 0 and (s - 10) // CT < NCH:
                    q = (s - 10) // CT
                    act.wait_ge(keptT_used, TB * (q + 1))
                    wait(act, att_back, q)
                    copy(attT[:], (side_ps, prep_ps)[q % 2][:]).then_inc(attT_done, 1)
                if 0 <= u + 1 < NCH * TB:
                    kept_hi(u + 1)
                if s < NT:
                    exp(s)
                if s == 15:
                    x_hi(0, NCH)
                if s == 16:
                    logit_copy(NCH)
                if s == 18:
                    tanh(NCH)
            act.wait_ge(keptT_used, NCH * TB)
            ffn_start(NCH)
            ffn(1)

        @block.gpsimd
        def _(pool):
            gp = nc.gpsimd

            def rstd(norm, C):
                pool.wait_ge(norm.var_done, C + 1)
                gp.tensor_tensor(norm.var_eps[:], norm.mean_var[:, :, 1], eps[:], ALU.add).then_inc(norm.eps_done, 1)
                pool.wait_ge(norm.eps_done, C + 1)
                gp.tensor_tensor(norm.rstd[:], norm.var_eps[:], neg_half[:], ALU.pow).then_inc(norm.rstd_done, 1)

            def w_split_lo(e, w):
                if w == 1:
                    pool.wait_ge(w1_hi_done, e + 1)
                    gp.tensor_tensor(w1_lo[:, e, :], w1_raw[:, e, :], w1_hi[:, e, :], ALU.subtract).then_inc(w_lo_done, 1)
                else:
                    pool.wait_ge(w2_hi_done, e + 1)
                    tiles = slice(e * HT, (e + 1) * HT)
                    gp.tensor_tensor(w2_lo[:, tiles, :], w2_raw[:, tiles, :], w2_hi[:, tiles, :],
                                     ALU.subtract).then_inc(w_lo_done, 1)

            def add_expert(C, e):
                pool.wait_ge(gated, C * E + e + 1)
                wait(pool, y_sum_done, C * (E - 1) + e - 1)
                gp.tensor_tensor(y_sum[:], y_sum[:], y_gated[:, e % 2, :], ALU.add).then_inc(y_sum_done, 1)

            def a_natural_lo(c):
                pool.wait_ge(aN_hi_done, c + 1)
                gp.tensor_tensor(aN_lo[:, bass.ds(c * CT, CT), :], att_norm.y[:], aN_hi[:, bass.ds(c * CT, CT), :],
                                 ALU.subtract).then_inc(aN_lo_done, 1)

            def ffn_chunk(ph, c, first=False, last=False):
                C = ph * NCH + c
                att = ph == 0 and not first
                if not first:
                    add_expert(C - 1, E - 1)
                if not last:
                    rstd(ffn_norm, C + 1)
                if ph == 0 and first:
                    for e, w in ((1, 2), (2, 1), (2, 2), (3, 1), (3, 2)):
                        w_split_lo(e, w)
                if att:
                    rstd(att_norm, C - 1)
                add_expert(C, 1)
                if att:
                    a_natural_lo(c - 1)
                add_expert(C, 2)

            def ffn(ph):
                ffn_chunk(ph, 0, first=True)
                with pool.Fori(1, NCH - 1) as c:
                    ffn_chunk(ph, c)
                ffn_chunk(ph, NCH - 1, last=True)
                add_expert(ph * NCH + NCH - 1, E - 1)

            gp.memset(ident[:], 0.0).then_inc(zeroed, 1)
            gp.memset(neg_half[:], -0.5).then_inc(zeroed, 1)
            gp.memset(eps[:], LN_EPS).then_inc(zeroed, 1)
            pool.wait_ge(zeroed, 3)
            gp.affine_select(out=ident[:], in_=ident[:], compare_op=ALU.not_equal, fill=1.0, base=0,
                             pattern=[[-1, P]], channel_multiplier=1).then_inc(ident_done, 1)
            gp.memset(before[:], 0.0).then_inc(zeroed, 1)
            gp.memset(wr_pad[:].bitcast(F32), 0.0).then_inc(wr_zero, 1)
            rstd(ffn_norm, 0)
            pool.wait_ge(zeroed, 4)
            for e in range(1, E):
                gp.memset(before[:, e, 0:e], 1.0).then_inc(before_done, 1)
            w_split_lo(0, 2)
            w_split_lo(1, 1)
            ffn(0)
            rstd(att_norm, NCH - 1)
            a_natural_lo(NCH - 1)
            rstd(ffn_norm, NCH)
            ffn(1)

        @block.vector
        def _(dve):
            ve = nc.vector

            def norm_stats(norm, c):
                for t in range(CT):
                    last = ve.bn_stats(norm.stats[:, t, :], X[:, c * CT + t, :])
                last.then_inc(norm.stats_done, 1)

            def norm_var(norm):
                for t in range(CT):
                    last = ve.bn_aggr(norm.mean_var[:, t, :], norm.stats[:, t, :])
                last.then_inc(norm.var_done, 1)

            def normalise(norm, c, C):
                dve.wait_ge(norm.rstd_done, C + 1)
                for t in range(CT):
                    last = ve.tensor_scalar(norm.y[:, t, :], X[:, c * CT + t, :], norm.mean_var[:, t, 0:1],
                                            norm.rstd[:, t:t + 1], ALU.subtract, ALU.mult)
                last.then_inc(norm.y_done, 1)

            def x_lo(c, C):
                dve.wait_ge(xT_hi_done, C + 1)
                ve.tensor_tensor(chunk(xT_lo, c), prep_ps[:], chunk(xT_hi, c), ALU.subtract).then_inc(xT_lo_done, 1)

            def a_natural_hi(c):
                dve.wait_ge(att_norm.y_done, c + 1)
                ve.tensor_copy(aN_hi[:, bass.ds(c * CT, CT), :], att_norm.y[:]).then_inc(aN_hi_done, 1)

            def a_lo(c, ps):
                dve.wait_ge(aT_hi_done, c + 1)
                ve.tensor_tensor(chunk(aT_lo, c), ps[:], chunk(aT_hi, c), ALU.subtract).then_inc(aT_lo_done, 1)

            def pairs(a, own):
                return a[:].unsqueeze(3 if own else 2).to_broadcast([P, CT, E, E])

            def router_rank(C):
                dve.wait_ge(logitT_ps, C + 1)
                n = ROUTER_OPS * C
                ps = prep_ps[:, 0:CT * 2 * E].rearrange("p (t e) -> p t e", t=CT)
                ve.tensor_tensor(logits_lo[:], ps[:, :, E:2 * E], br_all[:].unsqueeze(1).to_broadcast([P, CT, E]),
                                 ALU.add).then_inc(router, 1)
                dve.wait_ge(router, n + 1)
                ve.tensor_tensor(logits[:], ps[:, :, 0:E], logits_lo[:], ALU.add).then_inc(router, 1)
                dve.wait_ge(router, n + 2)
                ve.tensor_tensor(greater[:], pairs(logits, False), pairs(logits, True), ALU.is_gt).then_inc(router, 1)
                ve.tensor_tensor(equal[:], pairs(logits, False), pairs(logits, True), ALU.is_equal).then_inc(router, 1)
                dve.wait_ge(router, n + 4)
                flat = equal[:].rearrange("p t e f -> p t (e f)")
                ve.tensor_tensor(flat, flat, before[:].rearrange("p e f -> p (e f)").unsqueeze(1)
                                 .to_broadcast([P, CT, E * E]), ALU.mult).then_inc(router, 1)

            def router_choice(C):
                n = ROUTER_OPS * C
                dve.wait_ge(router, n + 5)
                ve.tensor_tensor(greater[:], greater[:], equal[:], ALU.add).then_inc(router, 1)
                dve.wait_ge(router, n + 6)
                ve.tensor_reduce(rank[:], greater[:], AX.X, ALU.add).then_inc(router, 1)
                dve.wait_ge(router, n + 7)
                ve.tensor_scalar(taken[:], rank[:], TOP_K - 0.5, None, ALU.is_lt).then_inc(router, 1)
                ve.scalar_tensor_tensor(out=taken_logits[:], in0=rank[:], scalar=TOP_K - 0.5, in1=logits[:],
                                        op0=ALU.is_lt, op1=ALU.mult).then_inc(router, 1)
                dve.wait_ge(router, n + 9)
                ve.tensor_reduce(taken_sum[:], taken_logits[:], AX.X, ALU.add).then_inc(router, 1)
                dve.wait_ge(router, n + 10)
                ve.scalar_tensor_tensor(out=tanh_in[:], in0=taken_sum[:].unsqueeze(2).to_broadcast([P, CT, E]),
                                        scalar=-0.5, in1=logits[:], op0=ALU.mult, op1=ALU.add).then_inc(router, 1)

            def router_gates(C):
                dve.wait_ge(tanh_done, C + 1)
                n = ROUTER_OPS * C
                ve.scalar_tensor_tensor(out=gates[:], in0=tanh_out[:], scalar=1.0, in1=taken[:], op0=ALU.add,
                                        op1=ALU.mult).then_inc(router, 1)
                dve.wait_ge(router, n + 12)
                ve.tensor_copy(gate_parts[:, :, 0:E].bitcast(F32R), gates[:]).then_inc(router, 1)
                dve.wait_ge(router, n + 13)
                ve.tensor_tensor(gate_parts[:, :, E:2 * E], gates[:], gate_parts[:, :, 0:E],
                                 ALU.subtract).then_inc(router, 1)

            def lo(C, k):
                dve.wait_ge(h_gelu, C * K + k + 1)
                wait(dve, h_used, C * K + k - NBUF + 1)
                b = k % NBUF
                ve.tensor_tensor(h_lo[:, b, :], h_full[:, b, :], h_hi[:, b, :], ALU.subtract).then_inc(h_lo_done, 1)

            def gate(C, e):
                dve.wait_ge(h_used, C * K + (e + 1) * HT)
                dve.wait_ge(gate_all_done, C * E + e + 1)
                if e == 0:
                    wait(dve, back_ps, C)
                if e == E - 1:
                    dve.wait_ge(y_sum_done, C * (E - 1) + E - 3)
                dst = y_sum[:] if e == 0 else y_gated[:, e % 2, :]
                mul = ve.scalar_tensor_tensor(out=dst, in0=y_ps[:, e % 2, :], scalar=y_shift[:, e:e + 1],
                                              in1=gate_all[:, e % 2, :], op0=ALU.add, op1=ALU.mult)
                mul.then_inc(gated, 1)

            def residual(c, C):
                dve.wait_ge(back_ps, C + 1)
                ve.scalar_tensor_tensor(out=x_tiles(c), in0=side_ps[:].rearrange("p (t d) -> p t d", t=CT),
                                        scalar=0.25, in1=x_tiles(c), op0=ALU.mult, op1=ALU.add).then_inc(resid_done, 1)

            def threshold(s):
                dve.wait_ge(exp_done, s + 1)
                ve.tensor_scalar(Z_thresh[:, s:s + 1], Z[:, s:s + 1], THRESH, None, ALU.mult).then_inc(thresh_done, 1)

            def keep(s):
                dve.wait_ge(thresh_done, s + 1)
                q = s // CT
                wait(dve, keptT_ps, TB * (q - 1))
                ve.scalar_tensor_tensor(out=kept[:, s % (2 * CT), :], in0=expS[:, s % NEXP, :],
                                        scalar=Z_thresh[:, s:s + 1], in1=expS[:, s % NEXP, :], op0=ALU.is_ge,
                                        op1=ALU.mult, accum_out=kept_sum[:, s:s + 1]).then_inc(kept_done, 1)

            def ffn_chunk(ph, c, first=False, last=False):
                C = ph * NCH + c
                att = ph == 0 and not first
                for k in range(K):
                    if k == 0:
                        router_gates(C)
                    if k == 0 and not first:
                        gate(C - 1, E - 1)
                    if k == 0 and first and ph == 0:
                        for later in range(1, NCH):
                            dve.wait_ge(x_in[later], 16)
                    if k == 1 and not last:
                        dve.wait_ge(ffn_norm.stats_done, C + 2)
                    if k == 5 and not first:
                        residual(c - 1, C - 1)
                    if k > HT and k % HT == 1:
                        gate(C, k // HT - 1)
                    if k == 6 and att:
                        dve.wait_ge(resid_done, C)
                    if k == 7 and att:
                        dve.wait_ge(att_norm.stats_done, C)
                    if k == 6 and first and ph == 0:
                        dve.wait_ge(w_sum_ps, 1)
                        ve.tensor_scalar(w_sum_all[:], side_ps[:, 0:D], 0.01, None, ALU.mult).then_inc(w_sum_all_done, 1)
                    if k == 8 and not last:
                        x_lo(c + 1, C + 1)
                    if k == 11 and att:
                        a_natural_hi(c - 1)
                    if k == 15 and att:
                        a_lo(c - 1, side_ps)
                    if k + LAG < K:
                        lo(C, k + LAG)
                    elif not last:
                        lo(C + 1, k + LAG - K)
                    if k == 0 and not last:
                        norm_stats(ffn_norm, c + 1)
                    if k == 1 and not last:
                        norm_var(ffn_norm)
                    if k == 3 and not last:
                        wait(dve, xT_ps, C + 1)
                        normalise(ffn_norm, c + 1, C + 1)
                    if k == 6 and att:
                        norm_stats(att_norm, c - 1)
                    if k == 7 and att:
                        norm_var(att_norm)
                    if k == 10 and att:
                        wait(dve, aT_ps, C - 1)
                        wait(dve, aN_lo_done, C - 1)
                        normalise(att_norm, c - 1, C - 1)
                    if k == 12 and not last:
                        router_rank(C + 1)
                    if k == 13 and not last:
                        router_choice(C + 1)

            def ffn(ph):
                ffn_chunk(ph, 0, first=True)
                with dve.Fori(1, NCH - 1) as c:
                    ffn_chunk(ph, c)
                ffn_chunk(ph, NCH - 1, last=True)

            dve.wait_ge(x_in[0], 16)
            norm_stats(ffn_norm, 0)
            dve.wait_ge(ffn_norm.stats_done, 1)
            norm_var(ffn_norm)
            dve.wait_ge(w1_hi_done, 1)
            ve.tensor_tensor(w1_lo[:, 0, :], w1_raw[:, 0, :], w1_hi[:, 0, :], ALU.subtract).then_inc(w1_lo0_done, 1)
            normalise(ffn_norm, 0, 0)
            dve.wait_ge(gelu_b1_done, 1)
            ve.tensor_copy(bias_cols[:], side_ps[:, 0:K + E]).then_inc(bias_col_done, 1)
            dve.wait_ge(wr_in, 16)
            dve.wait_ge(wr_zero, 1)
            ve.tensor_copy(wr_pad[:, 0:E], wr_raw[:]).then_inc(wr_hi_done, 1)
            dve.wait_ge(wr_hi_done, 1)
            ve.tensor_tensor(wr_pad[:, E:2 * E], wr_raw[:], wr_pad[:, 0:E], ALU.subtract).then_inc(wr_done, 1)
            x_lo(0, 0)
            dve.wait_ge(ident_done, 1)
            for e in range(E):
                last = ve.tensor_tensor(gate_sel[:, e, :], ident[0:2 * E, e:e + 1].to_broadcast([2 * E, P]),
                                        ident[0:2 * E, E + e:E + e + 1].to_broadcast([2 * E, P]), ALU.add)
            last.then_inc(sel_done, 1)
            dve.wait_ge(before_done, E - 1)
            dve.wait_ge(br_in, 16)
            lo(0, 0)
            router_rank(0)
            router_choice(0)
            lo(0, 1)
            dve.wait_ge(c_ps, 1)
            dve.wait_ge(bias_col_done, 1)
            ve.tensor_tensor(c_exp[:], side_ps[:, 0:E], b2_col, ALU.add).then_inc(c_step, 1)
            dve.wait_ge(c_step, 1)
            ve.tensor_reduce(c_sum[:], c_exp[:], AX.X, ALU.add).then_inc(c_step, 1)
            ve.tensor_tensor(c_neg[:], b2_col, c_exp[:], ALU.subtract).then_inc(c_step, 1)
            dve.wait_ge(c_step, 3)
            ve.tensor_scalar(y_shift[:], c_neg[:], c_sum[:], None, ALU.add).then_inc(c_step, 1)
            dve.wait_ge(W_in, 16)
            ve.tensor_reduce(w_sum[:], W_raw[:], AX.X, ALU.add).then_inc(w_sum_done, 1)
            dve.wait_ge(c_step, 4)
            lo(0, 2)
            ffn(0)

            def kept_lo(u):
                dve.wait_ge(keptT_hi_done, u + 1)
                wait(dve, keptT_used, u - NBUF + 1)
                ve.tensor_tensor(keptT_lo[:, u % NBUF, :], y_ps[:, u % 2, :], keptT_hi[:, u % NBUF, :],
                                 ALU.subtract).then_inc(keptT_lo_done, 1)

            def attention_sums(q):
                rows = slice(q * CT, (q + 1) * CT)
                dve.wait_ge(kept_done, CT * (q + 1))
                n = 4 * q
                ve.reciprocal(inv_Z[:], Z[:, rows]).then_inc(att_small, 1)
                ve.tensor_tensor(vac[:], Z[:, rows], kept_sum[:, rows], ALU.subtract).then_inc(att_small, 1)
                ve.scalar_tensor_tensor(out=den[:], in0=Z[:, rows], scalar=SUM_EPS, in1=kept_sum[:, rows],
                                        op0=ALU.mult, op1=ALU.add).then_inc(att_small, 1)
                dve.wait_ge(att_small, n + 3)
                ve.tensor_tensor(vac[:], vac[:], inv_Z[:], ALU.mult)
                ve.reciprocal(inv_den[:], den[:]).then_inc(att_small, 1)
                dve.wait_ge(att_small, n + 4)

            def attention_vacuum(q):
                for t in range(CT):
                    xt = X[:, q * CT + t, :]
                    last = ve.scalar_tensor_tensor(out=xt, in0=w_sum_all[:], scalar=vac[:, t:t + 1], in1=xt,
                                                   op0=ALU.mult, op1=ALU.add)
                last.then_inc(att_vac, 1)

            def attention_out(q):
                dve.wait_ge(att_vac, q + 1)
                dve.wait_ge(att_back, q + 1)
                for t in range(CT):
                    xt = X[:, q * CT + t, :]
                    last = ve.scalar_tensor_tensor(out=xt, in0=(side_ps, prep_ps)[q % 2][:, t * P:(t + 1) * P], scalar=inv_den[:, t:t + 1],
                                                   in1=xt, op0=ALU.mult, op1=ALU.add)
                last.then_inc(att_out, 1)

            for s in range(EARLY, NT + 7):
                u = 2 * (s - CT - 1)
                if s == EARLY:
                    threshold(0)
                    keep(0)
                    gate(NCH - 1, E - 1)
                    threshold(1)
                    keep(1)
                if s == 7:
                    a_lo(NCH - 1, prep_ps)
                if s == 18:
                    router_rank(NCH)
                if s == 6:
                    dve.wait_ge(aT_ps, NCH - 1)
                    dve.wait_ge(aN_lo_done, NCH - 1)
                    normalise(att_norm, NCH - 1, NCH - 1)
                    a_natural_hi(NCH - 1)
                if EARLY < s <= NT:
                    threshold(s - 1)
                if 0 <= u < NCH * TB:
                    kept_lo(u)
                if EARLY < s <= NT:
                    keep(s - 1)
                if s == 4:
                    residual(NCH - 1, NCH - 1)
                    dve.wait_ge(resid_done, NCH)
                    norm_stats(att_norm, NCH - 1)
                    dve.wait_ge(att_norm.stats_done, NCH)
                    norm_var(att_norm)
                if 0 <= u + 1 < NCH * TB:
                    kept_lo(u + 1)
                if s == 11:
                    dve.wait_ge(att_out, 1)
                    norm_stats(ffn_norm, 0)
                    dve.wait_ge(ffn_norm.stats_done, NCH + 1)
                    norm_var(ffn_norm)
                if s == 13:
                    dve.wait_ge(xT_ps, NCH)
                    normalise(ffn_norm, 0, NCH)
                if s == 16:
                    x_lo(0, NCH)
                if s == 18:
                    router_choice(NCH)
                if s >= 10 and (s - 10) % CT == 0 and (s - 10) // CT < NCH:
                    attention_out((s - 10) // CT)
                if s >= 7 and (s - 7) % CT == 0 and (s - 7) // CT < NCH:
                    attention_sums((s - 7) // CT)
                if s >= 8 and (s - 8) % CT == 0 and (s - 8) // CT < NCH:
                    attention_vacuum((s - 8) // CT)
            dve.wait_ge(att_out, NCH)
            dve.wait_ge(keptT_used, NCH * TB)
            for k in range(LAG):
                lo(NCH, k)
            ffn(1)
            gate(2 * NCH - 1, E - 1)
            residual(NCH - 1, 2 * NCH - 1)


_INS = ['L0_attn_x', 'L0_attn_W', 'L0_ffn_w1', 'L0_ffn_b1', 'L0_ffn_w2', 'L0_ffn_b2', 'L0_ffn_wr', 'L0_ffn_br']


def kernel(**inputs):
    import numpy as _np
    import concourse.bacc as _bacc
    from concourse import mybir as _mybir
    from concourse.bass_utils import run_bass_kernel_spmd as _run

    nc = _bacc.Bacc("TRN2", target_bir_lowering=False, num_devices=1)
    arrays, args = {}, []
    for name in _INS:
        a = _np.ascontiguousarray(inputs[name])
        arrays[f"in_{name}"] = a
        args.append(nc.dram_tensor(f"in_{name}", a.shape, _mybir.dt.from_np(a.dtype), kind="ExternalInput").ap())
    shape = inputs['L0_attn_x'].shape
    args.append(nc.dram_tensor("out_0", shape, _mybir.dt.float32, kind="ExternalOutput").ap())
    build(nc, *args)
    r = _run(nc, [arrays], core_ids=[0])
    return r.results[0]["out_0"]
```
